# Optimizing a Trainium2 kernel written in Bass

```python
import numpy as np
import jax
import jax.numpy as jnp

def _softmax(x, axis=-1):
    return jax.nn.softmax(x, axis=axis)

def _gelu(x):
    return jax.nn.gelu(x, approximate=True)

def _silu(x):
    return jax.nn.silu(x)

def _sigmoid(x):
    return jax.nn.sigmoid(x)

def _layernorm(x, axis=-1, eps=1e-05):
    m = jnp.mean(x, axis=axis, keepdims=True)
    v = jnp.var(x, axis=axis, keepdims=True)
    return (x - m) / jnp.sqrt(v + eps)

def _scatter_add(tgt, idx, src, axis=0):
    return tgt.at[idx].add(src)

def _segment_sum(src, seg, n):
    return jax.ops.segment_sum(src, seg, n)
kernel_name = 'mk_seq_preln_d2_jaxref_r8_16e28b'

def setup_inputs(seed: int=0):
    np.random.seed(seed)
    _w = jnp.asarray

    def _L0_attn_setup():
        import jax, jax.numpy as jnp
        import numpy as np
        NUM_HEAD = 16
        HIDDEN = 128
        HEAD_DIM = HIDDEN // NUM_HEAD
        key = jax.random.key(seed)
        k1, k2, k3, k4, k5 = jax.random.split(key, 5)
        scale = 0.02
        x = jax.random.normal(k1, (2, 256, HIDDEN), dtype=jnp.float32)
        w_in = jax.random.normal(k2, (3 * HIDDEN, HIDDEN), dtype=jnp.float32) * scale
        b_in = jax.random.normal(k3, (3 * HIDDEN,), dtype=jnp.float32) * scale
        w_out = jax.random.normal(k4, (HIDDEN, HIDDEN), dtype=jnp.float32) * scale
        b_out = jax.random.normal(k5, (HIDDEN,), dtype=jnp.float32) * scale
        return {'x': x, 'w_in': w_in, 'b_in': b_in, 'w_out': w_out, 'b_out': b_out}
    _L0_attn_in = _L0_attn_setup()

    def _L0_ffn_setup():
        import jax, jax.numpy as jnp
        import numpy as np
        E = 8
        D = 128
        DO = 128
        R = 64
        H = 32
        B, T = (8, 256)
        key = jax.random.key(seed)
        ks = jax.random.split(key, 12)
        s = lambda k, shape, fan: jax.random.normal(k, shape, jnp.float32) / np.sqrt(fan)
        return {'x': jax.random.normal(ks[0], (B, T, D), jnp.float32), 'W_base': s(ks[1], (D, DO), D), 'b_base': jnp.zeros((DO,), jnp.float32), 'Wd1': s(ks[2], (E, D, H), D), 'bd1': jnp.zeros((E, H), jnp.float32), 'Wd2': s(ks[3], (E, H, D), H), 'bd2': jnp.zeros((E, D), jnp.float32), 'Wa_down': s(ks[4], (E, D, R), D), 'ba_down': jnp.zeros((E, R), jnp.float32), 'Wa_up': s(ks[5], (E, R, DO), R), 'ba_up': jnp.zeros((E, DO), jnp.float32)}
    _L0_ffn_in = _L0_ffn_setup()

    def _L1_attn_setup():
        import jax, jax.numpy as jnp
        import numpy as np
        N_EMBD = 128
        N_HEAD = 16
        HEAD_DIM = N_EMBD // N_HEAD

        def _rope_tables(T, dim):
            inv_freq = 1.0 / 10000.0 ** (jnp.arange(0, dim, 2, dtype=jnp.float32) / dim)
            t = jnp.arange(T, dtype=jnp.float32)
            freqs = jnp.einsum('i,j->ij', t, inv_freq)
            emb = jnp.concatenate([freqs, freqs], axis=-1)
            return (jnp.cos(emb), jnp.sin(emb))

        def _apply_rope(x, cos, sin):
            x1, x2 = jnp.split(x, 2, axis=-1)
            rotated = jnp.concatenate([-x2, x1], axis=-1)
            return x * cos + rotated * sin
        key = jax.random.key(seed)
        k1, k2, k3 = jax.random.split(key, 3)
        B, T = (4, 256)
        scale = 1.0 / np.sqrt(N_EMBD)
        x = jax.random.normal(k1, (B, T, N_EMBD), dtype=jnp.float32)
        W_attn = jax.random.normal(k2, (N_EMBD, 3 * N_EMBD), dtype=jnp.float32) * scale
        W_proj = jax.random.normal(k3, (N_EMBD, N_EMBD), dtype=jnp.float32) * scale
        return {'x': x, 'W_attn': W_attn, 'W_proj': W_proj}
    _L1_attn_in = _L1_attn_setup()

    def _L1_ffn_setup():
        import jax, jax.numpy as jnp
        import numpy as np
        DIM = 128

        def _reference_tuple_inner(x, W_r, W_k, W_v, mu_r, mu_k):
            B, T, C = x.shape
            x_prev = jnp.concatenate([jnp.zeros((B, 1, C), x.dtype), x[:, :-1, :]], axis=1)
            xr = mu_r * x + (1.0 - mu_r) * x_prev
            xk = mu_k * x + (1.0 - mu_k) * x_prev
            r = jax.nn.sigmoid(jnp.einsum('btc,dc->btd', xr, W_r))
            k = jnp.einsum('btc,dc->btd', xk, W_k)
            k_act = jnp.square(jax.nn.relu(k))
            out = r * jnp.einsum('btc,dc->btd', k_act, W_v)
            new_state = x[:, -1, :]
            return (out, new_state)
        key = jax.random.key(seed)
        ks = jax.random.split(key, 6)
        B, T, C = (8, 256, DIM)
        x = jax.random.normal(ks[0], (B, T, C), dtype=jnp.float32)
        s = 1.0 / np.sqrt(C)
        W_r = jax.random.uniform(ks[1], (C, C), jnp.float32, -s, s)
        W_k = jax.random.uniform(ks[2], (C, C), jnp.float32, -s, s)
        W_v = jax.random.uniform(ks[3], (C, C), jnp.float32, -s, s)
        mu_r = jax.random.uniform(ks[4], (C,), jnp.float32)
        mu_k = jax.random.uniform(ks[5], (C,), jnp.float32)
        return {'x': x, 'W_r': W_r, 'W_k': W_k, 'W_v': W_v, 'mu_r': mu_r, 'mu_k': mu_k}
    _L1_ffn_in = _L1_ffn_setup()
    _d = {'L0_attn_x': _L0_attn_in['x'], 'L0_attn_w_in': _L0_attn_in['w_in'], 'L0_attn_b_in': _L0_attn_in['b_in'], 'L0_attn_w_out': _L0_attn_in['w_out'], 'L0_attn_b_out': _L0_attn_in['b_out'], 'L0_ffn_W_base': _L0_ffn_in['W_base'], 'L0_ffn_b_base': _L0_ffn_in['b_base'], 'L0_ffn_Wd1': _L0_ffn_in['Wd1'], 'L0_ffn_bd1': _L0_ffn_in['bd1'], 'L0_ffn_Wd2': _L0_ffn_in['Wd2'], 'L0_ffn_bd2': _L0_ffn_in['bd2'], 'L0_ffn_Wa_down': _L0_ffn_in['Wa_down'], 'L0_ffn_ba_down': _L0_ffn_in['ba_down'], 'L0_ffn_Wa_up': _L0_ffn_in['Wa_up'], 'L0_ffn_ba_up': _L0_ffn_in['ba_up'], 'L1_attn_W_attn': _L1_attn_in['W_attn'], 'L1_attn_W_proj': _L1_attn_in['W_proj'], 'L1_ffn_W_r': _L1_ffn_in['W_r'], 'L1_ffn_W_k': _L1_ffn_in['W_k'], 'L1_ffn_W_v': _L1_ffn_in['W_v'], 'L1_ffn_mu_r': _L1_ffn_in['mu_r'], 'L1_ffn_mu_k': _L1_ffn_in['mu_k']}
    _x0 = _d['L0_attn_x']
    _d['L0_attn_x'] = jax.random.normal(jax.random.fold_in(jax.random.key(seed), 1), (32, 256, 128), dtype=_x0.dtype)
    del _x0
    return _d

def reference(L0_attn_x, L0_attn_w_in, L0_attn_b_in, L0_attn_w_out, L0_attn_b_out, L0_ffn_W_base, L0_ffn_b_base, L0_ffn_Wd1, L0_ffn_bd1, L0_ffn_Wd2, L0_ffn_bd2, L0_ffn_Wa_down, L0_ffn_ba_down, L0_ffn_Wa_up, L0_ffn_ba_up, L1_attn_W_attn, L1_attn_W_proj, L1_ffn_W_r, L1_ffn_W_k, L1_ffn_W_v, L1_ffn_mu_r, L1_ffn_mu_k):

    def _L0_attn_ref(x, w_in, b_in, w_out, b_out):
        import jax, jax.numpy as jnp
        import numpy as np
        NUM_HEAD = 16
        HIDDEN = 128
        HEAD_DIM = HIDDEN // NUM_HEAD
        B, S, D = x.shape
        qkv = x @ w_in.T + b_in
        q, k, v = jnp.split(qkv, 3, axis=-1)

        def heads(t):
            return t.reshape(B, S, NUM_HEAD, HEAD_DIM).transpose(0, 2, 1, 3)
        q, k, v = (heads(q), heads(k), heads(v))
        scores = jnp.einsum('bhqd,bhkd->bhqk', q, k) / jnp.sqrt(jnp.asarray(HEAD_DIM, dtype=x.dtype))
        attn = jax.nn.softmax(scores, axis=-1)
        out = jnp.einsum('bhqk,bhkd->bhqd', attn, v)
        out = out.transpose(0, 2, 1, 3).reshape(B, S, D)
        return out @ w_out.T + b_out

    def _L0_ffn_ref(x, W_base, b_base, Wd1, bd1, Wd2, bd2, Wa_down, ba_down, Wa_up, ba_up):
        import jax, jax.numpy as jnp
        import numpy as np
        E = 8
        D = 128
        DO = 128
        R = 64
        H = 32
        B, T = (8, 256)
        base = jnp.einsum('btd,do->bto', x, W_base) + b_base
        h = jax.nn.relu(jnp.einsum('btd,edh->ebth', x, Wd1) + bd1[:, None, None, :])
        recon = jnp.einsum('ebth,ehd->ebtd', h, Wd2) + bd2[:, None, None, :]
        losses = jnp.mean((recon - x[None]) ** 2, axis=(2, 3))
        idx = jnp.argmin(losses, axis=0)
        a = jax.nn.relu(jnp.einsum('btd,bdr->btr', x, Wa_down[idx]) + ba_down[idx][:, None, :])
        adapter_out = jnp.einsum('btr,bro->bto', a, Wa_up[idx]) + ba_up[idx][:, None, :]
        return base + adapter_out

    def _L1_attn_ref(x, W_attn, W_proj):
        import jax, jax.numpy as jnp
        import numpy as np
        N_EMBD = 128
        N_HEAD = 16
        HEAD_DIM = N_EMBD // N_HEAD

        def _rope_tables(T, dim):
            inv_freq = 1.0 / 10000.0 ** (jnp.arange(0, dim, 2, dtype=jnp.float32) / dim)
            t = jnp.arange(T, dtype=jnp.float32)
            freqs = jnp.einsum('i,j->ij', t, inv_freq)
            emb = jnp.concatenate([freqs, freqs], axis=-1)
            return (jnp.cos(emb), jnp.sin(emb))

        def _apply_rope(x, cos, sin):
            x1, x2 = jnp.split(x, 2, axis=-1)
            rotated = jnp.concatenate([-x2, x1], axis=-1)
            return x * cos + rotated * sin
        B, T, C = x.shape
        H, D = (N_HEAD, HEAD_DIM)
        qkv = x @ W_attn
        q, k, v = jnp.split(qkv, 3, axis=-1)
        q = q.reshape(B, T, H, D).transpose(0, 2, 1, 3)
        k = k.reshape(B, T, H, D).transpose(0, 2, 1, 3)
        v = v.reshape(B, T, H, D).transpose(0, 2, 1, 3)
        cos, sin = _rope_tables(T, D)
        q = _apply_rope(q, cos, sin)
        k = _apply_rope(k, cos, sin)
        att = jnp.einsum('bhqd,bhkd->bhqk', q, k) * (1.0 / np.sqrt(D))
        causal = jnp.tril(jnp.ones((T, T), dtype=bool))
        att = jnp.where(causal, att, -jnp.inf)
        att = jax.nn.softmax(att, axis=-1)
        y = jnp.einsum('bhqk,bhkd->bhqd', att, v)
        y = y.transpose(0, 2, 1, 3).reshape(B, T, C)
        return y @ W_proj

    def _L1_ffn_ref(x, W_r, W_k, W_v, mu_r, mu_k):
        import jax, jax.numpy as jnp
        import numpy as np
        DIM = 128

        def _reference_tuple_inner(x, W_r, W_k, W_v, mu_r, mu_k):
            B, T, C = x.shape
            x_prev = jnp.concatenate([jnp.zeros((B, 1, C), x.dtype), x[:, :-1, :]], axis=1)
            xr = mu_r * x + (1.0 - mu_r) * x_prev
            xk = mu_k * x + (1.0 - mu_k) * x_prev
            r = jax.nn.sigmoid(jnp.einsum('btc,dc->btd', xr, W_r))
            k = jnp.einsum('btc,dc->btd', xk, W_k)
            k_act = jnp.square(jax.nn.relu(k))
            out = r * jnp.einsum('btc,dc->btd', k_act, W_v)
            new_state = x[:, -1, :]
            return (out, new_state)
        return _reference_tuple_inner(x, W_r, W_k, W_v, mu_r, mu_k)[0]
    x = L0_attn_x
    x = x + _L0_attn_ref(_layernorm(x, axis=-1), L0_attn_w_in, L0_attn_b_in, L0_attn_w_out, L0_attn_b_out)
    x = x + _L0_ffn_ref(_layernorm(x, axis=-1), L0_ffn_W_base, L0_ffn_b_base, L0_ffn_Wd1, L0_ffn_bd1, L0_ffn_Wd2, L0_ffn_bd2, L0_ffn_Wa_down, L0_ffn_ba_down, L0_ffn_Wa_up, L0_ffn_ba_up)
    x = x + _L1_attn_ref(_layernorm(x, axis=-1), L1_attn_W_attn, L1_attn_W_proj)
    x = x + _L1_ffn_ref(_layernorm(x, axis=-1), L1_ffn_W_r, L1_ffn_W_k, L1_ffn_W_v, L1_ffn_mu_r, L1_ffn_mu_k)
    return x

_drawn_inputs = setup_inputs


def setup_inputs(seed=0):
    import zlib

    import numpy as np

    out = dict(_drawn_inputs(seed))
    spreads = {'L0_ffn_b_base': (0.0, 0.1),
     'L0_ffn_bd1': (0.0, 0.1),
     'L0_ffn_bd2': (0.0, 0.1),
     'L0_ffn_ba_down': (0.0, 0.1),
     'L0_ffn_ba_up': (0.0, 0.1)}
    factors = {'L1_ffn_W_r': 4.267, 'L1_ffn_mu_r': 8.0}
    for name, (base, spread) in spreads.items():
        noise = np.random.default_rng([zlib.crc32(name.encode()), seed]).standard_normal(out[name].shape)
        drawn = base * np.exp(spread * noise) if base else spread * noise
        out[name] = jnp.asarray(drawn.astype(out[name].dtype))
    for name, factor in factors.items():
        out[name] = (out[name] * factor).astype(out[name].dtype)
    return out
```

```python
import concourse.bass as bass
from concourse import mybir
from contextlib import ExitStack

F32, BF16, U32 = mybir.dt.float32, mybir.dt.bfloat16, mybir.dt.uint32
ALU, ACT, AX = mybir.AluOpType, mybir.ActivationFunctionType, mybir.AxisListType

NB, T, D = 32, 256, 128
P = 128
NT = T // P
H, HD = 16, 8
NPART = 3
KROWS = NPART * NPART * HD
MROWS = NPART
NBUF = 3
EPS = 1e-5


class Seq:

    def __init__(self, const, turn=None, per_turn=0):
        self.const, self.turn, self.per_turn = const, turn, per_turn

    def __add__(self, k):
        return Seq(self.const + k, self.turn, self.per_turn)

    def __sub__(self, k):
        return self + -k

    def times(self, n, more=0):
        value = self.const * n + more
        return value if self.turn is None else self.turn * (self.per_turn * n) + value


def live(b):
    return b.turn is not None or 0 <= b.const < NB


def begun(b):
    return b.turn is not None or b.const >= 0


def upto(b, per=1, more=None):
    if b.turn is None and b.const >= NB:
        b, more = Seq(NB - 1), None
    return b.times(per, per if more is None else more)


def upto_in_buffer(b, nbuf, per):
    turns = b.const // nbuf
    return (turns + 1) * per if b.turn is None else b.turn * per + (turns + 1) * per


def run_steps(eng, step, first, last, behind=2, ahead=3, nbuf=NBUF):
    n = (NB - ahead - behind) // nbuf * nbuf
    for s in range(first, behind):
        step(Seq(s), s % nbuf)
    with eng.Fori(0, n // nbuf) as i:
        for k in range(nbuf):
            step(Seq(behind + k, i, nbuf), (behind + k) % nbuf)
    for s in range(behind + n, last + 1):
        step(Seq(s), s % nbuf)


def attention(nc, name, x_sb, x_loaded, w, causal):
    if causal:
        a_chunks = [(0, range(4 * c, 4 * c + 4), P) for c in range(4)]
        a_chunks += [(1, range(2 * c, 2 * c + 2), T) for c in range(8)]
    else:
        a_chunks = [(qt, range(2 * c, 2 * c + 2), T) for qt in range(NT) for c in range(8)]
    b_chunks, group_last = [], []
    for region in range(2):
        for ab in range(2):
            for kt in range(NT):
                if causal and kt == 1:
                    b_chunks.append((region, ab, kt, range(4), P))
                else:
                    b_chunks += [(region, ab, kt, range(2), 0), (region, ab, kt, range(2, 4), 0)]
                group_last.append(len(b_chunks) - 1)
    NA, NBC, NG = len(a_chunks), len(b_chunks), len(group_last)
    NP = 6 if causal else 8
    assert NBC % NP == 0 and NA % 2 == 0 and NBC % 2 == 0
    ROUND_SLOT = 4 if causal else 3
    group_of = [next(g for g in range(NG) if group_last[g] >= c) for c in range(NBC)]
    a_slots = [[] for _ in range(NBC)]
    for c in range(NA):
        a_slots[c * 3 // 4 if not causal else c * 5 // 6].append(c)
    pv_slots, pv_tail = [[] for _ in range(NBC)], []
    for g in range(NG):
        at = group_last[g] + 3
        (pv_slots[at] if at < NBC else pv_tail).append(g)

    scratch = nc.dram_tensor(f"{name}_scratch", (NBUF, 3 * NPART - 1, P, T), BF16).ap()
    ctx = ExitStack()
    with ctx:
        def sb(nm, shape, dt=F32):
            return ctx.enter_context(nc.sbuf_tensor(f"{name}_{nm}", shape, dt))

        def sem(nm):
            return ctx.enter_context(nc.semaphore(f"{name}_{nm}"))

        stats = sb("stats", [P, NBUF, NT, 6])
        meanvar = sb("meanvar", [P, NBUF, NT, 2])
        vareps = sb("vareps", [P, NBUF, NT])
        rstd = sb("rstd", [P, NBUF, NT])
        xn = sb("xn", [P, NBUF, NT, D])
        xnT = sb("xnT", [P, NBUF, T])
        qk = sb("qk", [P, NBUF, 2, T])
        roped = sb("roped", [P, 2, 2, T]) if causal else None
        resid = sb("resid", [P, 2, T])
        parts = sb("parts", [P, NBUF, 2 * NPART, T], BF16)
        qstack = sb("qstack", [P, NBUF, H * T], BF16)
        kstack = sb("kstack", [P, NBUF, H * T], BF16)
        vpad = sb("vpad", [P, NBUF, NT, H * 32])
        negmax = sb("negmax", [P, NBUF, NT, H])
        mresid = sb("mresid", [P, NT, H])
        mparts = sb("mparts", [P, NBUF, NT, NPART, H], BF16)
        maxT = sb("maxT", [NPART * H, NBUF, T], BF16)
        probs = sb("probs", [P, NP, 2 * T])
        outT = sb("outT", [P, NBUF, 2 * T])
        recip = sb("recip", [P, NBUF, NT * H])
        recip16 = sb("recip16", [P, 2 * NT, P])
        outTn = sb("outTn", [P, NBUF, 2 * T])

        def bank(nm):
            return ctx.enter_context(nc.psum_tensor(f"{name}_{nm}", [P, 512], F32))

        bank_a = [bank("a0"), bank("a1")]
        bank_b = [bank("b0"), bank("b1")]
        bank_o = [bank("o0"), bank("o1")]
        m0, m1 = bank("m0"), bank("m1")
        maxT_ps = m1[0:NPART * H, 0:T // 2].bitcast(BF16)

        stats_done, meanvar_done, vareps_done, rstd_done, xn_done = map(
            sem, ("stats_done", "meanvar_done", "vareps_done", "rstd_done", "xn_done"))
        xnT_in_m0, xnT_ready = sem("xnT_in_m0"), sem("xnT_ready")
        q_in_m1, k_in_m0, qk_moved, qk_ready = sem("q_in_m1"), sem("k_in_m0"), sem("qk_moved"), sem("qk_ready")
        v_in_psum, v_ready = sem("v_in_psum"), sem("v_ready")
        part_rounded, part_taken, parts_ready, stacks_loaded = map(
            sem, ("part_rounded", "part_taken", "parts_ready", "stacks_loaded"))
        a_scored, a_maxed = sem("a_scored"), sem("a_maxed")
        msplit_step, mparts_ready, maxT_in_m1, maxT_ready, maxrow_loaded = map(
            sem, ("msplit_step", "mparts_ready", "maxT_in_m1", "maxT_ready", "maxrow_loaded"))
        b_scored, exp_done, probs_ready = sem("b_scored"), sem("exp_done"), sem("probs_ready")
        if not causal:
            probs_ready = exp_done
        pv_done, out_moved = sem("pv_done"), sem("out_moved")
        recip_spread = sem("recip_spread")
        den_in_m0, recip_done, recip_in_m0, normed = map(sem, ("den_in_m0", "recip_done", "recip_in_m0", "normed"))
        y_in_psum, x_updated, consts_set = sem("y_in_psum"), sem("x_updated"), sem("consts_set")

        def stack_rows(n, which):
            ap = scratch[n, which * NPART, :, :]
            return bass.AP(ap.tensor, ap.offset,
                           [[which * P * T, NPART], [H * T, NPART * HD], [1, H * T]])

        def strided_pairs(pairs):
            ap = pairs[:, :, 0:HD]
            dims = [list(x) for x in ap.ap]
            return bass.AP(ap.tensor, ap.offset, [dims[0], dims[1], [48, 2], dims[2]])

        parts_stored = sem("parts_stored")
        NSTACK = 2
        apart = sem("apart")
        block = ctx.enter_context(nc.Block())

        @block.sync
        def _(sp):
            def step(s, r):
                b, n = s + 2, (r + 2) % NBUF
                if live(b):
                    sp.wait_ge(parts_ready, upto(b))
                    sp.sem_inc(apart, 1)
                    if begun(b - NBUF):
                        sp.wait_ge(b_scored, upto(b - NBUF, NBC))
                        sp.sem_inc(apart, 1)
                    for slot, first, count in ((0, 0, 2 * NPART), (2 * NPART, NPART, NPART - 1)):
                        sp.dma_start(scratch[n, slot:slot + count, :, :].rearrange("a p t -> p a t"),
                                     parts[:, n, first:first + count, :]).then_inc(parts_stored, 16)
                    sp.wait_ge(parts_stored, b.times(32, 32))
                    sp.dma_start(qstack[0:KROWS, n, :], stack_rows(n, 0)).then_inc(stacks_loaded, 16)
                    sp.dma_start(kstack[0:KROWS, n, :], stack_rows(n, 1)).then_inc(stacks_loaded, 16)
                b, n = s + 1, (r + 1) % NBUF
                if live(b):
                    sp.wait_ge(maxT_ready, upto(b))
                    sp.sem_inc(apart, 1)
                    dst = qstack[KROWS:KROWS + MROWS, n, :].rearrange("p (h t) -> p h t", h=H)
                    sp.dma_start(dst, maxT[:, n, :]).then_inc(maxrow_loaded, 16)
            sp.wait_ge(consts_set, 4)
            run_steps(sp, step, -2, NB - 2)

        @block.gpsimd
        def _(pool):
            nc.gpsimd.memset(kstack[64:P, :, :], 1.0).then_inc(consts_set, 1)
            pool.wait_ge(consts_set, 1)
            nc.gpsimd.memset(vpad[:, :, :, :], 0.0).then_inc(consts_set, 1)
            pool.wait_ge(consts_set, 2)
            pairs = vpad[:, :, :, :].rearrange("p n t (g u) -> p (n t) g u", u=64)
            nc.gpsimd.memset(pairs[:, :, :, 8:16], 1.0).then_inc(consts_set, 1)
            nc.gpsimd.memset(pairs[:, :, :, 56:64], 1.0).then_inc(consts_set, 1)

            def mask(b, c):
                region, ab, kt, groups, q0 = b_chunks[c]
                pool.wait_ge(exp_done, upto(b, NBC, c + 1))
                pool.sem_inc(apart, 1)
                n = len(groups)
                tile = probs[:, c % NP, :].rearrange("p (g q) -> p g q", g=n)[:, :, 0:P]
                nc.gpsimd.affine_select(out=tile, in_=tile, compare_op=ALU.is_ge, fill=0.0, base=0,
                                        pattern=[[0, n], [1, P]], channel_multiplier=-1)\
                    .then_inc(probs_ready, 1)

            def split(s, r):
                b, n = s + 2, (r + 2) % NBUF
                if not live(b):
                    return
                if causal:
                    for i in range(2):
                        pool.wait_ge(qk_moved, upto(b, 2, i + 1))
                        nc.gpsimd.tensor_tensor(qk[:, n, i, :], roped[:, i, 0, :], roped[:, i, 1, :], ALU.add)\
                            .then_inc(qk_ready, 1)
                src, p = qk[:, n, :, :], [parts[:, n, i::NPART, :] for i in range(NPART)]
                pool.wait_ge(part_rounded, upto(b, 2, 1))
                nc.gpsimd.tensor_tensor(resid[:, :, :], src, p[0], ALU.subtract).then_inc(part_taken, 1)
                pool.wait_ge(part_rounded, upto(b, 2))
                nc.gpsimd.tensor_tensor(p[2], resid[:, :, :], p[1], ALU.subtract).then_inc(parts_ready, 1)

            def inverse_spread(s, r):
                b, n = s + 3, r
                if live(b):
                    pool.wait_ge(meanvar_done, upto(b, NT))
                    pool.sem_inc(apart, 1)
                    nc.gpsimd.tensor_scalar(vareps[:, n, :], meanvar[:, n, :, 1], EPS, None, ALU.add).then_inc(vareps_done, 1)
                    pool.wait_ge(vareps_done, b.times(1, 1))
                    pool.sem_inc(apart, 1)
                    nc.gpsimd.tensor_tensor(rstd[:, n, :], vareps[:, n, :], w["neghalf"][:, 0:NT], ALU.pow)\
                        .then_inc(rstd_done, 1)

            def split_max(s, r):
                b, n = s + 1, (r + 1) % NBUF
                if not live(b):
                    return
                pool.wait_ge(a_maxed, upto(b, NA))
                pool.sem_inc(apart, 1)
                m = [mparts[:, n, :, i, :] for i in range(NPART)]
                src = negmax[:, n, :, :]
                nc.gpsimd.tensor_copy(m[0], src).then_inc(msplit_step, 1)
                pool.wait_ge(msplit_step, b.times(3, 1))
                pool.sem_inc(apart, 1)
                nc.gpsimd.tensor_tensor(mresid[:, :, :], src, m[0], ALU.subtract).then_inc(msplit_step, 1)
                pool.wait_ge(msplit_step, b.times(3, 2))
                pool.sem_inc(apart, 1)
                nc.gpsimd.tensor_copy(m[1], mresid[:, :, :]).then_inc(msplit_step, 1)
                pool.wait_ge(msplit_step, b.times(3, 3))
                pool.sem_inc(apart, 1)
                nc.gpsimd.tensor_tensor(m[2], mresid[:, :, :], m[1], ALU.subtract).then_inc(mparts_ready, 1)

            def step(s, r):
                for c in range(NBC):
                    if causal and live(s):
                        mask(s, c)
                    if c == 4:
                        split(s, r)
                    if c == NBC - 4:
                        inverse_spread(s, r)
                    if c == NBC - 1:
                        split_max(s, r)
            run_steps(pool, step, -3, NB)

        @block.scalar
        def _(act):
            def move_out(b, n, region):
                if live(b):
                    act.wait_ge(pv_done, upto(b, NG, (region + 1) * NG // 2))
                    nc.scalar.activation(outT[:, n, region * T:(region + 1) * T], bank_o[region][:, 0:T],
                                         ACT.Copy).then_inc(out_moved, 1)

            def step(s, r):
                move_out(s - 1, (r - 1) % NBUF, 1)
                b, n = s + 2, (r + 2) % NBUF
                if live(b):
                    act.wait_ge(xnT_in_m0, upto(b))
                    nc.scalar.activation(xnT[:, n, :], m0[:, 0:T], ACT.Copy).then_inc(xnT_ready, 1)
                for c in range(NBC):
                    if live(s):
                        act.wait_ge(b_scored, upto(s, NBC, c + 1))
                        if c >= NP:
                            act.wait_ge(pv_done, upto(s, NG, group_of[c - NP] + 1))
                        else:
                            if begun(s - 1):
                                act.wait_ge(pv_done, upto(s - 1, NG, group_of[c - NP + NBC] + 1))
                        nc.scalar.activation(probs[:, c % NP, :], bank_b[c % 2][:, :], ACT.Exp)\
                            .then_inc(exp_done, 1)
                    if c == 2 and live(b) and not causal:
                        act.wait_ge(q_in_m1, upto(b))
                        nc.scalar.activation(qk[:, n, 0, :], m1[:, 0:T], ACT.Identity, bias=w["bq_scaled"][:, :],
                                             scale=float(HD) ** -0.5).then_inc(qk_ready, 1)
                        nc.scalar.activation(qk[:, n, 1, :], m1[:, T:2 * T], ACT.Identity, bias=w["bk"][:, :])\
                            .then_inc(qk_ready, 1)
                    if c == 4 and live(b) and causal:
                        act.wait_ge(v_in_psum, upto(b))
                        for t in range(NT):
                            dst = strided_pairs(vpad[:, n, t, :].rearrange("p (g u) -> p g u", u=64))
                            src = m0[:, t * P:(t + 1) * P].rearrange("p (g a d) -> p g a d", a=2, d=HD)
                            nc.scalar.activation(dst, src, ACT.Copy).then_inc(v_ready, 1)
                    if c == ROUND_SLOT and live(b):
                        act.wait_ge(qk_ready, upto(b, 2))
                        if begun(b - NBUF):
                            act.wait_ge(parts_stored, upto(b - NBUF, 32))
                        nc.scalar.activation(parts[:, n, 0::NPART, :], qk[:, n, :, :], ACT.Copy)\
                            .then_inc(part_rounded, 1)
                    if c == 7 and live(s - 1):
                        act.wait_ge(recip_done, upto(s - 1))
                        if begun(s - 2):
                            act.wait_ge(recip_in_m0, upto(s - 2))
                        ap = recip[:, (r - 1) % NBUF, :]
                        each16 = bass.AP(ap.tensor, ap.offset, [*[list(x) for x in ap.ap], [0, 16]])
                        nc.scalar.activation(recip16[:, :, :].rearrange("p a (h c) -> p (a h) c", c=16), each16,
                                             ACT.Copy).then_inc(recip_spread, 1)
                    if c == ROUND_SLOT + 2 and live(b):
                        act.wait_ge(part_taken, upto(b))
                        nc.scalar.activation(parts[:, n, 1::NPART, :], resid[:, :, :], ACT.Copy)\
                            .then_inc(part_rounded, 1)
                    if c == group_last[NG // 2 - 1] + 4:
                        move_out(s, r, 0)
                b, n = s + 1, (r + 1) % NBUF
                if live(b):
                    act.wait_ge(maxT_in_m1, upto(b))
                    nc.scalar.activation(maxT[:, n, :], maxT_ps, ACT.Copy).then_inc(maxT_ready, 1)
            run_steps(act, step, -2, NB)

        @block.vector
        def _(dve):
            def maxima(b, n, c):
                if live(b):
                    qt, heads, keys = a_chunks[c]
                    dve.wait_ge(a_scored, upto(b, NA, c + 1))
                    nc.vector.tensor_reduce(
                        out=negmax[:, n, qt, heads[0]:heads[-1] + 1],
                        in_=bank_a[c % 2][:, :].rearrange("p (h k) -> p h k", k=keys),
                        axis=AX.X, op=ALU.max, negate=True).then_inc(a_maxed, 1)

            def spread(s, r):
                b, n = s + 3, r
                if live(b):
                    for t in range(NT):
                        nc.vector.bn_stats(stats[:, n, t, :], x_sb[:, bass.ds(b.times(T, t * P), P)])\
                            .then_inc(stats_done, 1)
                    dve.wait_ge(stats_done, upto(b, NT))
                    dve.sem_inc(apart, 1)
                    for t in range(NT):
                        nc.vector.bn_aggr(meanvar[:, n, t, :], stats[:, n, t, :]).then_inc(meanvar_done, 1)

            def centre(s, r):
                b, n = s + 3, r
                if live(b):
                    dve.wait_ge(rstd_done, upto(b))
                    if begun(b - NBUF):
                        dve.wait_ge(xnT_in_m0, upto(b - NBUF))
                    for t in range(NT):
                        nc.vector.tensor_scalar(xn[:, n, t, :], x_sb[:, bass.ds(b.times(T, t * P), P)],
                                                meanvar[:, n, t, 0:1], rstd[:, n, t:t + 1],
                                                ALU.subtract, ALU.mult).then_inc(xn_done, 1)

            def rope(s, r, i):
                b = s + 2
                if live(b) and causal:
                    dve.wait_ge((q_in_m1, k_in_m0)[i], upto(b))
                    if begun(b - 1):
                        dve.wait_ge(qk_ready, upto(b - 1, 2))
                    nc.vector.tensor_tensor(roped[:, i, :, :], (m1, m0)[i][:, :].rearrange("p (a t) -> p a t", a=2),
                                            w["rope"][:, i, :, :], ALU.mult).then_inc(qk_moved, 1)

            def value(s, r):
                b, n = s + 2, (r + 2) % NBUF
                if live(b) and not causal:
                    dve.wait_ge(v_in_psum, upto(b))
                    for t in range(NT):
                        dst = strided_pairs(vpad[:, n, t, :].rearrange("p (g u) -> p g u", u=64))
                        src = m0[:, t * P:(t + 1) * P].rearrange("p (g a d) -> p g a d", a=2, d=HD)
                        bias = w["bv"][:, :].rearrange("p (g a d) -> p g a d", a=2, d=HD)
                        nc.vector.tensor_tensor(dst, src, bias, ALU.add).then_inc(v_ready, 1)

            def invert(s, r):
                b, n = s - 1, (r - 1) % NBUF
                if live(b):
                    dve.wait_ge(den_in_m0, upto(b))
                    nc.vector.reciprocal(recip[:, n, :], m0[:, 0:NT * H]).then_inc(recip_done, 1)

            def normalise(s, r):
                b, n = s - 1, (r - 1) % NBUF
                if live(b):
                    dve.wait_ge(recip_in_m0, upto(b))
                    nc.vector.tensor_tensor(outTn[:, n, :], m0[:, :], outT[:, n, :], ALU.mult).then_inc(normed, 1)

            def update(s, r):
                b = s - 1
                if live(b):
                    dve.wait_ge(y_in_psum, upto(b))
                    tile = x_sb[:, bass.ds(b.times(T), T)]
                    nc.vector.tensor_tensor(tile, m1[:, 0:T], tile, ALU.add).then_inc(x_updated, 1)

            def step(s, r):
                b, n = s + 1, (r + 1) % NBUF
                for c in range(NA):
                    if c == 3:
                        rope(s, r, 0)
                    if c == 4:
                        rope(s, r, 1)
                    if c == 6:
                        value(s, r)
                    if c == 7:
                        invert(s, r)
                    if c == 9:
                        normalise(s, r)
                    if c == NA - 1:
                        spread(s, r)
                    maxima(b, n, c)
                update(s, r)
                centre(s, r)
            dve.wait_ge(consts_set, 4)
            if x_loaded is not None:
                dve.wait_ge(x_loaded, 32)
            run_steps(dve, step, -3, NB)

        @block.tensor
        def _(pe):
            def score_a(b, n, c):
                if not live(b):
                    return
                if c == 0:
                    pe.wait_ge(stacks_loaded, upto(b, 16 * NSTACK))
                qt, heads, keys = a_chunks[c]
                if c >= 2:
                    pe.wait_ge(a_maxed, upto(b, NA, c - 1))
                else:
                    if begun(b - 1):
                        pe.wait_ge(a_maxed, upto(b - 1, NA, NA + c - 1))
                ps = bank_a[c % 2]
                if causal:
                    masked = ps[:, :].rearrange("p (h k) -> p h k", k=keys)[:, :, keys - P:keys]
                    nc.tensor.matmul(masked, w["ident_bf"][:, :], w["mask"][:, 0:len(heads), :],
                                     start=True, stop=False, skip_group_check=True)
                for i, h in enumerate(heads):
                    last = nc.tensor.matmul(
                        ps[:, i * keys:(i + 1) * keys],
                        qstack[0:KROWS, n, h * T + qt * P:h * T + qt * P + P],
                        kstack[0:KROWS, n, h * T:h * T + keys],
                        start=not causal, stop=True, skip_group_check=causal)
                last.then_inc(a_scored, 1)

            def score_b(b, n, c):
                if not live(b):
                    return
                if c == 0:
                    pe.wait_ge(maxrow_loaded, upto(b, 16))
                region, ab, kt, groups, q0 = b_chunks[c]
                if c >= 2:
                    pe.wait_ge(exp_done, upto(b, NBC, c - 1))
                else:
                    if begun(b - 1):
                        pe.wait_ge(exp_done, upto(b - 1, NBC, NBC + c - 1))
                nq = T - q0
                for i, j in enumerate(groups):
                    h = region * 8 + j * 2 + ab
                    last = nc.tensor.matmul(
                        bank_b[c % 2][:, i * nq:(i + 1) * nq],
                        kstack[0:KROWS + MROWS, n, h * T + kt * P:h * T + kt * P + P],
                        qstack[0:KROWS + MROWS, n, h * T + q0:(h + 1) * T], start=True, stop=True)
                last.then_inc(b_scored, 1)

            def weigh(b, n, g):
                if not live(b):
                    return
                if g == 0:
                    pe.wait_ge(v_ready, upto(b, NT))
                region, ab, kt, groups, q0 = b_chunks[group_last[g]]
                if g % (NG // 2) == 0:
                    if begun(b - 1):
                        pe.wait_ge(out_moved, upto(b - 1, 2, region + 1))
                pe.wait_ge(probs_ready, upto(b, NBC, group_last[g] + 1))
                nq = T - q0
                for j in range(4):
                    h = region * 8 + j * 2 + ab
                    c = next(c for c in range(NBC) if b_chunks[c][:3] == (region, ab, kt) and j in b_chunks[c][3])
                    i = j - b_chunks[c][3][0]
                    last = nc.tensor.matmul(
                        bank_o[region][32 * j:32 * j + 32, q0:T],
                        vpad[:, n, kt, h * 32:(h + 1) * 32],
                        probs[:, c % NP, i * nq:(i + 1) * nq],
                        start=(g % (NG // 2) == 0), stop=(g % (NG // 2) == NG // 2 - 1))
                last.then_inc(pv_done, 1)

            def transpose_x(s, r):
                b, n = s + 2, (r + 2) % NBUF
                if live(b):
                    pe.wait_ge(xn_done, upto(b, NT))
                    if begun(s - 2):
                        pe.wait_ge(normed, upto(s - 2))
                    if begun(b - 1):
                        pe.wait_ge(v_ready, upto(b - 1, NT))
                    for t in range(NT):
                        last = nc.tensor.transpose(m0[:, t * P:(t + 1) * P], xn[:, n, t, :], w["ident"][:, :])
                    last.then_inc(xnT_in_m0, 1)

            def project_q(s, r):
                b, n = s + 2, (r + 2) % NBUF
                if live(b):
                    pe.wait_ge(xnT_ready, upto(b))
                    if begun(s - 2):
                        pe.wait_ge(x_updated, upto(s - 2))
                    if begun(s):
                        pe.wait_ge(maxT_ready, upto(s))
                    nc.tensor.matmul(m1[:, 0:T], w["wq"][:, :], xnT[:, n, :], start=True, stop=True)
                    nc.tensor.matmul(m1[:, T:2 * T], w["wqrot" if causal else "wk"][:, :], xnT[:, n, :],
                                     start=True, stop=True).then_inc(q_in_m1, 1)

            def project_k(s, r):
                b, n = s + 2, (r + 2) % NBUF
                if live(b) and causal:
                    nc.tensor.matmul(m0[:, 0:T], w["wk"][:, :], xnT[:, n, :], start=True, stop=True)
                    nc.tensor.matmul(m0[:, T:2 * T], w["wkrot"][:, :], xnT[:, n, :],
                                     start=True, stop=True).then_inc(k_in_m0, 1)

            def project_v(s, r):
                b, n = s + 2, (r + 2) % NBUF
                if live(b):
                    if causal:
                        pe.wait_ge(qk_moved, upto(b, 2))
                    for t in range(NT):
                        last = nc.tensor.matmul(m0[:, t * P:(t + 1) * P], xnT[:, n, t * P:(t + 1) * P],
                                                w["wv"][:, :], start=True, stop=True)
                    last.then_inc(v_in_psum, 1)

            def pick_den(s, r):
                b, n = s - 1, (r - 1) % NBUF
                if live(b):
                    pe.wait_ge(out_moved, upto(b, 2))
                    pe.wait_ge(v_ready, upto(s + 2, NT))
                    for t in range(NT):
                        for region in range(2):
                            at = (t * 2 + region) * H // 2
                            last = nc.tensor.matmul(m0[:, at:at + H // 2],
                                                    outT[:, n, region * T + t * P:region * T + (t + 1) * P],
                                                    w["den_pick"][:, :], start=True, stop=True)
                    last.then_inc(den_in_m0, 1)

            def spread_recip(s, r):
                b, n = s - 1, (r - 1) % NBUF
                if live(b):
                    pe.wait_ge(recip_spread, upto(b))
                    for t in range(NT):
                        for region in range(2):
                            last = nc.tensor.transpose(m0[:, region * T + t * P:region * T + (t + 1) * P],
                                                       recip16[:, t * 2 + region, :], w["ident"][:, :])
                    last.then_inc(recip_in_m0, 1)

            def project_out(s, r):
                b, n = s - 1, (r - 1) % NBUF
                if live(b):
                    pe.wait_ge(normed, upto(b))
                    pe.wait_ge(qk_moved if causal else qk_ready, upto(s + 2, 2))
                    for t in range(NT):
                        for region in range(2):
                            last = nc.tensor.matmul(
                                m1[:, t * P:(t + 1) * P],
                                outTn[:, n, region * T + t * P:region * T + (t + 1) * P],
                                w["wo"][:, region, :], start=(region == 0), stop=(region == 1))
                    last.then_inc(y_in_psum, 1)

            def transpose_max(s, r):
                b, n = s + 1, (r + 1) % NBUF
                if live(b):
                    if begun(s - 1):
                        pe.wait_ge(x_updated, upto(s - 1))
                    pe.wait_ge(qk_moved if causal else qk_ready, upto(s + 2, 2))
                    pe.wait_ge(mparts_ready, upto(b))
                    pe.sem_inc(apart, 1)
                    for t in range(NT):
                        last = nc.tensor.transpose(
                            maxT_ps[:, t * P:(t + 1) * P],
                            mparts[:, n, t, :, :].rearrange("p a h -> p (a h)"), w["ident_bf"][:, :])
                    last.then_inc(maxT_in_m1, 1)

            def step(s, r):
                for g in pv_tail:
                    weigh(s - 1, (r - 1) % NBUF, g)
                for c in range(NBC):
                    if c == 0:
                        transpose_x(s, r)
                    if c == 2:
                        project_q(s, r)
                    if c == 3:
                        project_k(s, r)
                    if c == 4:
                        project_v(s, r)
                    if c == 5:
                        pick_den(s, r)
                    if c == 8:
                        spread_recip(s, r)
                    if c == 10:
                        project_out(s, r)
                    for a in a_slots[c]:
                        score_a(s + 1, (r + 1) % NBUF, a)
                    score_b(s, r, c)
                    for g in pv_slots[c]:
                        weigh(s, r, g)
                transpose_max(s, r)
            pe.wait_ge(consts_set, 4)
            run_steps(pe, step, -2, NB)


def expert_ffn(nc, x_sb, w, wa_down, ba_down, wa_up, ba_up):
    NBF = 5
    E, HE, R = 8, 32, 64
    XC, OC, H1C, HXW = P, 2 * P, 2 * P + 1, 3 * P + 1
    MC = 2 * P + 1
    ctx = ExitStack()
    with ctx:
        def sb(nm, shape, dt=F32):
            return ctx.enter_context(nc.sbuf_tensor(f"f0_{nm}", shape, dt))

        def sem(nm):
            return ctx.enter_context(nc.semaphore(f"f0_{nm}"))

        stats = sb("stats", [P, NBF, NT, 6])
        meanvar = sb("meanvar", [P, NBF, NT, 2])
        vareps = sb("vareps", [P, NBF, NT])
        rstd = sb("rstd", [P, NBF, NT])
        hx = sb("hx", [P, NBF, NT, HXW])
        xnT = sb("xnT", [P, NBF, T])
        xsum = sb("xsum", [P, NBF])
        hpre = sb("hpre", [P, NBF, NT, 2 * P])
        weighed = sb("weighed", [P, NBF, 2, MC])
        rowloss = sb("rowloss", [P, NBF, 2])
        negloss = sb("negloss", [1, NBF, E])
        best8 = sb("best8", [1, NBF, 8])
        best_at = sb("best_at", [1, NBF, 8], U32)
        wd_sel = sb("wd_sel", [P, NBF, R])
        bd_sel = sb("bd_sel", [R, NBF, 1])
        wu_sel = sb("wu_sel", [R + 2, NBF, D])
        hidT = sb("hidT", [R + 2, NBF, T])

        def bank(nm):
            return ctx.enter_context(nc.psum_tensor(f"f0_{nm}", [P, 512], F32))

        ps_x, ps_h, ps_g, ps_l, ps_d, ps_y = (bank("x"), bank("h"), [bank("g0"), bank("g1")], bank("l"),
                                             bank("d"), bank("y"))
        stats_done, meanvar_done, vareps_done, rstd_done, xn_done = map(
            sem, ("stats_done", "meanvar_done", "vareps_done", "rstd_done", "xn_done"))
        xnT_in_psum, xnT_ready, h_in_psum, h_biased, h_ready = map(
            sem, ("xnT_in_psum", "xnT_ready", "h_in_psum", "h_biased", "h_ready"))
        moments_in_psum, moments_weighed, loss_in_psum, loss_moved, best_found, expert_known = map(
            sem, ("moments_in_psum", "moments_weighed", "loss_in_psum", "loss_moved", "best_found",
                  "expert_known"))
        down_in_psum, hid_ready, y_in_psum, x_updated, consts_set = map(
            sem, ("down_in_psum", "hid_ready", "y_in_psum", "x_updated", "consts_set"))
        adapter_loaded = [sem(f"adapter_loaded{n}") for n in range(NBF)]
        base_loaded, apart = sem("base_loaded"), sem("apart")
        NCONST = 2
        block = ctx.enter_context(nc.Block())

        def steps(eng, step, first, last):
            run_steps(eng, step, first, last, behind=5, ahead=2, nbuf=NBF)

        @block.sync
        def _(sp):
            for n in range(NBF):
                sp.dma_start(wu_sel[R + 1:R + 2, n, :], w["b_base_dram"]).then_inc(base_loaded, 16)
            sp.wait_ge(base_loaded, 16 * NBF)

            def step(s, n):
                if not live(s):
                    return
                sp.wait_ge(expert_known, upto(s))
                sp.sem_inc(apart, 1)
                if begun(s - NBF):
                    sp.wait_ge(y_in_psum, upto(s - NBF))
                    sp.sem_inc(apart, 1)
                e = sp.value_load(best_at[0:1, n, 0:1], min_val=0, max_val=E - 1)
                sp.dma_start(wd_sel[:, n, :], wa_down[bass.ds(e * D, D), :]).then_inc(adapter_loaded[n], 16)
                sp.dma_start(bd_sel[:, n, :], ba_down[bass.ds(e * R, R), :]).then_inc(adapter_loaded[n], 16)
                sp.dma_start(wu_sel[0:R, n, :], wa_up[bass.ds(e * R, R), :]).then_inc(adapter_loaded[n], 16)
                sp.dma_start(wu_sel[R:R + 1, n, :], ba_up[bass.ds(e, 1), :]).then_inc(adapter_loaded[n], 16)
            steps(sp, step, 0, NB - 1)

        @block.gpsimd
        def _(pool):
            nc.gpsimd.memset(hx[:, :, :, OC:OC + 1], 1.0).then_inc(consts_set, 1)
            pool.wait_ge(consts_set, 1)
            nc.gpsimd.memset(hidT[R:R + 2, :, :], 1.0).then_inc(consts_set, 1)

            def step(s, n):
                b, n = s + 2, (n + 2) % NBF
                if live(b):
                    pool.wait_ge(meanvar_done, upto(b, NT))
                    pool.sem_inc(apart, 1)
                    nc.gpsimd.tensor_scalar(vareps[:, n, :], meanvar[:, n, :, 1], EPS, None, ALU.add)\
                        .then_inc(vareps_done, 1)
                    pool.wait_ge(vareps_done, upto(b))
                    nc.gpsimd.tensor_tensor(rstd[:, n, :], vareps[:, n, :], w["neghalf"][:, 0:NT], ALU.pow)\
                        .then_inc(rstd_done, 1)
            steps(pool, step, -2, NB - 3)

        @block.scalar
        def _(act):
            def step(s, r):
                b, n = s + 1, (r + 1) % NBF
                if live(b):
                    act.wait_ge(xnT_in_psum, upto(b))
                    nc.scalar.activation(xnT[:, n, :], ps_x[:, 0:T], ACT.Copy, accum_out=xsum[:, n:n + 1])\
                        .then_inc(xnT_ready, 1)
                b, n = s - 2, (r - 2) % NBF
                if live(b):
                    act.wait_ge(down_in_psum, upto(b))
                    nc.scalar.activation(hidT[0:R, n, :], ps_d[0:R, 0:T], ACT.Relu, bias=bd_sel[:, n, :])\
                        .then_inc(hid_ready, 1)
                b, n = s + 1, (r + 1) % NBF
                if live(b):
                    act.wait_ge(h_biased, upto(b))
                    if begun(b - NBF):
                        act.wait_ge(moments_in_psum, upto(b - NBF, 2))
                    for t in range(NT):
                        ap = hx[:, n, t, 0:P]
                        dims = [list(x) for x in ap.ap]
                        dst = bass.AP(ap.tensor, ap.offset, [dims[0], [H1C, 2], dims[1]])
                        nc.scalar.activation(dst, hpre[:, n, t, :].rearrange("p (g h) -> p g h", g=2),
                                             ACT.Relu).then_inc(h_ready, 1)
            act.wait_ge(consts_set, NCONST)
            steps(act, step, -1, NB + 1)

        @block.vector
        def _(dve):
            def norm(s, r):
                b, n = s + 2, (r + 2) % NBF
                if live(b):
                    for t in range(NT):
                        nc.vector.bn_stats(stats[:, n, t, :], x_sb[:, bass.ds(b.times(T, t * P), P)])\
                            .then_inc(stats_done, 1)
                    dve.wait_ge(stats_done, upto(b, NT))
                    dve.sem_inc(apart, 1)
                    for t in range(NT):
                        nc.vector.bn_aggr(meanvar[:, n, t, :], stats[:, n, t, :]).then_inc(meanvar_done, 1)

            def centre(s, r):
                b, n = s + 2, (r + 2) % NBF
                if live(b):
                    dve.wait_ge(rstd_done, upto(b))
                    if begun(b - NBF):
                        dve.wait_ge(moments_in_psum, upto(b - NBF, 2))
                    for t in range(NT):
                        nc.vector.tensor_scalar(hx[:, n, t, XC:XC + D], x_sb[:, bass.ds(b.times(T, t * P), P)],
                                                meanvar[:, n, t, 0:1], rstd[:, n, t:t + 1],
                                                ALU.subtract, ALU.mult).then_inc(xn_done, 1)

            def step(s, r):
                if live(s):
                    dve.wait_ge(moments_in_psum, upto(s, 2))
                    for g in range(2):
                        nc.vector.tensor_tensor_reduce(
                            out=weighed[:, r, g, :], in0=ps_g[g][:, 0:MC], in1=w["moment_weights"][:, g, :],
                            scale=1.0, scalar=0.0, op0=ALU.mult, op1=ALU.add,
                            accum_out=rowloss[:, r, g:g + 1]).then_inc(moments_weighed, 1)
                norm(s, r)
                b, n = s + 1, (r + 1) % NBF
                if live(b):
                    dve.wait_ge(h_in_psum, upto(b))
                    nc.vector.tensor_tensor(hpre[:, n, :, :], ps_h[:, :].rearrange("p (t h) -> p t h", t=NT),
                                            w["bd1"][:, :, :], ALU.add).then_inc(h_biased, 1)
                centre(s, r)
                if live(s):
                    dve.wait_ge(loss_in_psum, upto(s))
                    nc.vector.tensor_copy(negloss[:, r, :], ps_l[0:1, 0:E]).then_inc(loss_moved, 1)
                    dve.wait_ge(loss_moved, upto(s))
                    dve.sem_inc(apart, 1)
                    nc.vector.max(best8[:, r, :], negloss[:, r, :]).then_inc(best_found, 1)
                    dve.wait_ge(best_found, upto(s))
                    dve.sem_inc(apart, 1)
                    nc.vector.max_index(best_at[:, r, :], best8[:, r, :], negloss[:, r, :])\
                        .then_inc(expert_known, 1)
                b = s - 2
                if live(b):
                    dve.wait_ge(y_in_psum, upto(b))
                    tile = x_sb[:, bass.ds(b.times(T), T)]
                    nc.vector.tensor_tensor(tile, ps_y[:, 0:T], tile, ALU.add).then_inc(x_updated, 1)
            dve.wait_ge(consts_set, NCONST)
            steps(dve, step, -2, NB + 1)

        @block.tensor
        def _(pe):
            def step(s, r):
                b, n = s + 1, (r + 1) % NBF
                if live(b):
                    pe.wait_ge(xn_done, upto(b, NT))
                    if begun(b - 1):
                        pe.wait_ge(xnT_ready, upto(b - 1))
                    for t in range(NT):
                        last = nc.tensor.transpose(ps_x[:, t * P:(t + 1) * P], hx[:, n, t, XC:XC + D],
                                                   w["ident"][:, :])
                    last.then_inc(xnT_in_psum, 1)
                b, m = s - 2, (r - 2) % NBF
                if live(b):
                    pe.wait_ge(adapter_loaded[m], upto_in_buffer(b, NBF, 64))
                    if begun(b - 1):
                        pe.wait_ge(hid_ready, upto(b - 1))
                    nc.tensor.matmul(ps_d[0:R, 0:T], wd_sel[:, m, :], xnT[:, m, :], start=True, stop=True)\
                        .then_inc(down_in_psum, 1)
                if live(s):
                    pe.wait_ge(h_ready, upto(s, NT))
                    if begun(s - 1):
                        pe.wait_ge(moments_weighed, upto(s - 1, 2))
                    for g in range(2):
                        for t in range(NT):
                            last = nc.tensor.matmul(
                                ps_g[g][:, 0:MC], hx[:, r, t, g * H1C:g * H1C + P],
                                hx[:, r, t, g * P:g * P + MC], start=(t == 0), stop=(t == NT - 1))
                        last.then_inc(moments_in_psum, 1)
                if live(s + 1):
                    pe.wait_ge(xnT_ready, upto(s + 1))
                    pe.wait_ge(h_biased, upto(s))
                    for t in range(NT):
                        last = nc.tensor.matmul(ps_h[:, t * 2 * P:(t + 1) * 2 * P],
                                                xnT[:, n, t * P:(t + 1) * P], w["wd1"][:, :],
                                                start=True, stop=True)
                    last.then_inc(h_in_psum, 1)
                if live(b):
                    pe.wait_ge(hid_ready, upto(b))
                    if begun(b - 1):
                        pe.wait_ge(x_updated, upto(b - 1))
                    for t in range(NT):
                        nc.tensor.matmul(ps_y[:, t * P:(t + 1) * P], xnT[:, m, t * P:(t + 1) * P],
                                         w["w_base"][:, :], start=True, stop=False)
                        last = nc.tensor.matmul(ps_y[:, t * P:(t + 1) * P], hidT[:, m, t * P:(t + 1) * P],
                                                wu_sel[:, m, :], start=False, stop=True)
                    last.then_inc(y_in_psum, 1)
                if live(s):
                    pe.wait_ge(moments_weighed, upto(s, 2))
                    if begun(s - 1):
                        pe.wait_ge(loss_moved, upto(s - 1))
                    for g in range(2):
                        nc.tensor.matmul(ps_l[0:1, 0:E], rowloss[:, r, g:g + 1], w["neg_expert"][:, g, :],
                                         start=(g == 0), stop=False)
                    nc.tensor.matmul(ps_l[0:1, 0:E], xsum[:, r:r + 1], w["twice_bd2T"][:, :],
                                     start=False, stop=False)
                    nc.tensor.matmul(ps_l[0:1, 0:E], w["ones"][0:1, 0:1], w["neg_bias_loss"][:, :],
                                     start=False, stop=True).then_inc(loss_in_psum, 1)
            pe.wait_ge(consts_set, NCONST)
            steps(pe, step, -1, NB + 1)


def channel_mix(nc, x_sb, w, out):
    ctx = ExitStack()
    with ctx:
        def sb(nm, shape, dt=F32):
            return ctx.enter_context(nc.sbuf_tensor(f"f1_{nm}", shape, dt))

        def sem(nm):
            return ctx.enter_context(nc.semaphore(f"f1_{nm}"))

        def bank(nm):
            return ctx.enter_context(nc.psum_tensor(f"f1_{nm}", [P, 512], F32))

        stats = sb("stats", [P, NBUF, NT, 6])
        meanvar = sb("meanvar", [P, NBUF, NT, 2])
        vareps = sb("vareps", [P, NBUF, NT])
        rstd = sb("rstd", [P, NBUF, NT])
        xn = sb("xn", [P, NBUF, NT, D])
        xnT = sb("xnT", [P, NBUF, 1 + T])
        delta = sb("delta", [P, NBUF, T])
        mixed = sb("mixed", [P, NBUF, 2, T])
        tanh_r = sb("tanh_r", [P, NBUF, T])
        relu_k = sb("relu_k", [P, NBUF, T])
        k_act = sb("k_act", [P, NBUF, T])
        gated = sb("gated", [P, NBUF, T])
        ps_x, ps_r, ps_k, ps_v = bank("x"), bank("r"), bank("k"), bank("v")
        stats_done, meanvar_done, vareps_done, rstd_done, xn_done = map(
            sem, ("stats_done", "meanvar_done", "vareps_done", "rstd_done", "xn_done"))
        xnT_in_psum, xnT_ready, delta_ready, mixed_ready = map(
            sem, ("xnT_in_psum", "xnT_ready", "delta_ready", "mixed_ready"))
        r_in_psum, tanh_ready, k_in_psum, relu_ready, k_ready = map(
            sem, ("r_in_psum", "tanh_ready", "k_in_psum", "relu_ready", "k_ready"))
        v_in_psum, gated_ready, result_ready, stored, consts_set = map(
            sem, ("v_in_psum", "gated_ready", "result_ready", "stored", "consts_set"))
        apart = sem("apart")
        out_v = out.rearrange("(n p) d -> p n d", p=P)
        block = ctx.enter_context(nc.Block())

        def steps(eng, step, first, last):
            run_steps(eng, step, first, last, behind=2, ahead=2)

        @block.sync
        def _(sp):
            def step(s, r):
                b = s - 1
                if live(b):
                    sp.wait_ge(result_ready, upto(b))
                    sp.sem_inc(apart, 1)
                    src = x_sb[:, bass.ds(b.times(T), T)].rearrange("p (t d) -> p t d", t=NT)
                    sp.dma_start(out_v[:, bass.ds(b.times(NT), NT), :], src).then_inc(stored, 16)
            steps(sp, step, 1, NB)
            sp.wait_ge(stored, 16 * NB)

        @block.gpsimd
        def _(pool):
            nc.gpsimd.memset(xnT[:, :, 0:1], 0.0).then_inc(consts_set, 1)

            def step(s, r):
                b, n = s + 1, (r + 1) % NBUF
                if live(b):
                    pool.wait_ge(xnT_ready, upto(b))
                    nc.gpsimd.tensor_tensor(delta[:, n, :], xnT[:, n, 1:1 + T], xnT[:, n, 0:T], ALU.subtract)\
                        .then_inc(delta_ready, 1)
                b, n = s + 2, (r + 2) % NBUF
                if live(b):
                    pool.wait_ge(meanvar_done, upto(b, NT))
                    pool.sem_inc(apart, 1)
                    nc.gpsimd.tensor_scalar(vareps[:, n, :], meanvar[:, n, :, 1], EPS, None, ALU.add)\
                        .then_inc(vareps_done, 1)
                    pool.wait_ge(vareps_done, upto(b))
                    nc.gpsimd.tensor_tensor(rstd[:, n, :], vareps[:, n, :], w["neghalf"][:, 0:NT], ALU.pow)\
                        .then_inc(rstd_done, 1)
            steps(pool, step, -2, NB)

        @block.scalar
        def _(act):
            def step(s, r):
                b, n = s + 1, (r + 1) % NBUF
                if live(b):
                    act.wait_ge(xnT_in_psum, upto(b))
                    nc.scalar.activation(xnT[:, n, 1:1 + T], ps_x[:, 0:T], ACT.Copy).then_inc(xnT_ready, 1)
                if live(s):
                    act.wait_ge(k_in_psum, upto(s))
                    nc.scalar.activation(relu_k[:, r, :], ps_k[:, 0:T], ACT.Relu).then_inc(relu_ready, 1)
                    act.wait_ge(r_in_psum, upto(s))
                    nc.scalar.activation(tanh_r[:, r, :], ps_r[:, 0:T], ACT.Tanh, scale=0.5)\
                        .then_inc(tanh_ready, 1)
                    act.wait_ge(relu_ready, upto(s))
                    nc.scalar.activation(k_act[:, r, :], relu_k[:, r, :], ACT.Square).then_inc(k_ready, 1)
            act.wait_ge(consts_set, 1)
            steps(act, step, -1, NB)

        @block.vector
        def _(dve):
            def step(s, r):
                b, n = s + 2, (r + 2) % NBUF
                if live(b):
                    for t in range(NT):
                        nc.vector.bn_stats(stats[:, n, t, :], x_sb[:, bass.ds(b.times(T, t * P), P)])\
                            .then_inc(stats_done, 1)
                    dve.wait_ge(stats_done, upto(b, NT))
                    dve.sem_inc(apart, 1)
                    for t in range(NT):
                        nc.vector.bn_aggr(meanvar[:, n, t, :], stats[:, n, t, :]).then_inc(meanvar_done, 1)
                b, n = s - 1, (r - 1) % NBUF
                if live(b):
                    dve.wait_ge(v_in_psum, upto(b))
                    nc.vector.scalar_tensor_tensor(out=gated[:, n, :], in0=tanh_r[:, n, :], scalar=1.0,
                                                   in1=ps_v[:, 0:T], op0=ALU.add, op1=ALU.mult)\
                        .then_inc(gated_ready, 1)
                b, n = s + 1, (r + 1) % NBUF
                if live(b):
                    dve.wait_ge(delta_ready, upto(b))
                    for i, mu in enumerate(("mu_r", "mu_k")):
                        nc.vector.scalar_tensor_tensor(out=mixed[:, n, i, :], in0=delta[:, n, :],
                                                       scalar=w[mu][:, :], in1=xnT[:, n, 0:T],
                                                       op0=ALU.mult, op1=ALU.add).then_inc(mixed_ready, 1)
                b, n = s + 2, (r + 2) % NBUF
                if live(b):
                    dve.wait_ge(rstd_done, upto(b))
                    for t in range(NT):
                        nc.vector.tensor_scalar(xn[:, n, t, :], x_sb[:, bass.ds(b.times(T, t * P), P)],
                                                meanvar[:, n, t, 0:1], rstd[:, n, t:t + 1],
                                                ALU.subtract, ALU.mult).then_inc(xn_done, 1)
                b, n = s - 1, (r - 1) % NBUF
                if live(b):
                    dve.wait_ge(gated_ready, upto(b))
                    tile = x_sb[:, bass.ds(b.times(T), T)]
                    nc.vector.scalar_tensor_tensor(out=tile, in0=gated[:, n, :], scalar=0.5, in1=tile,
                                                   op0=ALU.mult, op1=ALU.add).then_inc(result_ready, 1)
            steps(dve, step, -2, NB)

        @block.tensor
        def _(pe):
            def step(s, r):
                b, n = s + 1, (r + 1) % NBUF
                if live(b):
                    pe.wait_ge(xn_done, upto(b, NT))
                    if begun(b - 1):
                        pe.wait_ge(xnT_ready, upto(b - 1))
                    for t in range(NT):
                        last = nc.tensor.transpose(ps_x[:, t * P:(t + 1) * P], xn[:, n, t, :], w["ident"][:, :])
                    last.then_inc(xnT_in_psum, 1)
                if live(s):
                    pe.wait_ge(mixed_ready, upto(s, 2))
                    if begun(s - 1):
                        pe.wait_ge(relu_ready, upto(s - 1))
                    nc.tensor.matmul(ps_k[:, 0:T], w["w_kT"][:, :], mixed[:, r, 1, :], start=True, stop=True)\
                        .then_inc(k_in_psum, 1)
                    if begun(s - 1):
                        pe.wait_ge(tanh_ready, upto(s - 1))
                    for t in range(NT):
                        last = nc.tensor.matmul(ps_r[:, t * P:(t + 1) * P], mixed[:, r, 0, t * P:(t + 1) * P],
                                                w["w_rT"][:, :], start=True, stop=True)
                    last.then_inc(r_in_psum, 1)
                b, n = s - 1, (r - 1) % NBUF
                if live(b):
                    pe.wait_ge(k_ready, upto(b))
                    if begun(b - 1):
                        pe.wait_ge(gated_ready, upto(b - 1))
                    for t in range(NT):
                        last = nc.tensor.matmul(ps_v[:, t * P:(t + 1) * P], k_act[:, n, t * P:(t + 1) * P],
                                                w["w_vT"][:, :], start=True, stop=True)
                    last.then_inc(v_in_psum, 1)
            pe.wait_ge(consts_set, 1)
            steps(pe, step, -1, NB)


def transformer_kernel(nc, a, out):
    E, HE = 8, 32
    ctx = ExitStack()
    with ctx:
        def sb(nm, shape, dt=F32):
            return ctx.enter_context(nc.sbuf_tensor(nm, shape, dt))

        x_sb = sb("x_sb", [P, NB * NT * D])
        x_loaded = ctx.enter_context(nc.semaphore("x_loaded"))
        w = {nm: sb(nm, shape) for nm, shape in (
            ("l0_wq", [P, P]), ("l0_wk", [P, P]), ("l0_wv", [P, P]), ("l0_wo", [P, 2, P]),
            ("l0_bq", [P, 1]), ("l0_bk", [P, 1]), ("l0_bv", [P, P]), ("l0_bq_scaled", [P, 1]),
            ("l1_wq", [P, P]), ("l1_wqrot", [P, P]), ("l1_wk", [P, P]), ("l1_wkrot", [P, P]),
            ("l1_wv", [P, P]), ("l1_wo", [P, 2, P]), ("rope", [P, 2, 2, T]),
            ("ident", [P, P]), ("mask_f", [P, P]), ("den_pick", [P, H // 2]), ("neghalf", [P, NT]), ("ones", [P, 1]),
            ("w_base", [P, D]), ("wd1", [P, E * HE]), ("bd1", [P, NT, E * HE]),
            ("wd2", [P, 2, D]), ("wd2T", [P, E * HE]), ("bd2T", [P, E]), ("block_mask", [P, P]),
            ("expert_of", [P, 2, E]),
            ("w_rT", [P, P]), ("w_kT", [P, P]), ("w_vT", [P, P]), ("mu_r", [P, 1]), ("mu_k", [P, 1]))}
        w["ident_bf"] = sb("ident_bf", [P, P], BF16)
        w["mask"] = sb("mask", [P, 4, P], BF16)
        w["moment_weights"] = sb("moment_weights", [P, 2, 2 * P + 1])
        w["neg_expert"] = sb("neg_expert", [P, 2, E])
        w["twice_bd2T"] = sb("twice_bd2T", [P, E])
        w["neg_bias_loss"] = sb("neg_bias_loss", [1, E])

        inner = ExitStack()
        with inner:
            bd2T_sq = inner.enter_context(nc.sbuf_tensor("bd2T_sq", [P, E], F32))
            w2b2 = inner.enter_context(nc.sbuf_tensor("w2b2", [P, 2, E], F32))
            w2b2_sum = inner.enter_context(nc.sbuf_tensor("w2b2_sum", [P, 2], F32))
            ps = [inner.enter_context(nc.psum_tensor(f"setup{i}", [P, 512], F32)) for i in range(4)]
            loaded, squared, products, tables = (inner.enter_context(nc.semaphore(nm)) for nm in
                                                 ("loaded", "squared", "products", "tables"))
            block = inner.enter_context(nc.Block())
            loads = [(w[nm][:], a[nm]) for nm in a["_names"]]
            for nm in ("l0_bv", "bd1"):
                row = a[nm + "_row"]
                n = row.shape[1]
                dst = w[nm]
                if nm == "bd1":
                    loads += [(dst[:, t, :], row.partition_broadcast(P)) for t in range(NT)]
                else:
                    loads.append((dst[:, :], row.partition_broadcast(P)))
            x_v = a["x"].rearrange("(n p) d -> p n d", p=P)
            x_t = x_sb[:, :].rearrange("p (n d) -> p n d", d=D)
            first = NBUF * NT

            @block.sync
            def _(sp):
                for dst, src in loads[0::2]:
                    sp.dma_start(dst, src).then_inc(loaded, 16)
                sp.dma_start(x_t[:, 0:first, :], x_v[:, 0:first, :]).then_inc(x_loaded, 16)
                sp.dma_start(x_t[:, first:, :], x_v[:, first:, :]).then_inc(x_loaded, 16)

            @block.scalar
            def _(act):
                for dst, src in loads[1::2]:
                    act.dma_start(dst, src).then_inc(loaded, 16)

            @block.vector
            def _(dve):
                dve.wait_ge(loaded, 16 * len(loads))
                nc.vector.tensor_tensor(bd2T_sq[:, :], w["bd2T"][:, :], w["bd2T"][:, :], ALU.mult)\
                    .then_inc(squared, 1)
                nc.vector.tensor_copy(w["ident_bf"][:, :], w["ident"][:, :])
                for i in range(4):
                    nc.vector.tensor_copy(w["mask"][:, i, :], w["mask_f"][:, :])
                nc.vector.tensor_scalar(w["l0_bq_scaled"][:, :], w["l0_bq"][:, :], float(HD) ** -0.5, None, ALU.mult)
                nc.vector.tensor_scalar(w["neg_expert"][:, :, :], w["expert_of"][:, :, :], -1.0, None, ALU.mult)
                nc.vector.tensor_scalar(w["twice_bd2T"][:, :], w["bd2T"][:, :], 2.0, None, ALU.mult)
                dve.wait_ge(products, 1)
                nc.vector.tensor_scalar(w["neg_bias_loss"][:, :], ps[3][0:1, 0:E], -float(T), None, ALU.mult)
                for g in range(2):
                    gram, cross, ones = ((0, P, 2 * P), (P + 1, 0, P))[g]
                    mw = w["moment_weights"]
                    nc.vector.tensor_tensor(mw[:, g, gram:gram + P], ps[g][:, 0:P], w["block_mask"][:, :], ALU.mult)
                    nc.vector.tensor_scalar(mw[:, g, cross:cross + P], w["wd2"][:, g, :], -2.0, None, ALU.mult)
                    nc.vector.tensor_tensor(w2b2[:, g, :], ps[2][:, g * E:(g + 1) * E], w["expert_of"][:, g, :],
                                            ALU.mult).then_inc(tables, 1)
                    dve.wait_ge(tables, 2 * g + 1)
                    nc.vector.tensor_reduce(out=w2b2_sum[:, g:g + 1], in_=w2b2[:, g, :], axis=AX.X, op=ALU.add)\
                        .then_inc(tables, 1)
                    dve.wait_ge(tables, 2 * g + 2)
                    nc.vector.tensor_scalar(mw[:, g, ones:ones + 1], w2b2_sum[:, g:g + 1], 2.0, None, ALU.mult)

            @block.tensor
            def _(pe):
                pe.wait_ge(loaded, 16 * len(loads))
                for g in range(2):
                    w2T = w["wd2T"][:, g * P:(g + 1) * P]
                    nc.tensor.matmul(ps[g][:, 0:P], w2T, w2T, start=True, stop=True)
                    nc.tensor.matmul(ps[2][:, g * E:(g + 1) * E], w2T, w["bd2T"][:, :], start=True, stop=True)
                pe.wait_ge(squared, 1)
                nc.tensor.matmul(ps[3][0:1, 0:E], w["ones"][:, :], bd2T_sq[:, :], start=True, stop=True)\
                    .then_inc(products, 1)

        shared = {nm: w[nm] for nm in ("ident", "ident_bf", "mask", "den_pick", "neghalf", "rope")}
        w["b_base_dram"] = a["b_base"]
        attention(nc, "a0", x_sb, x_loaded,
                  shared | {nm[3:]: w[nm] for nm in w if nm.startswith("l0_")}, causal=False)
        expert_ffn(nc, x_sb, w, a["wa_down"], a["ba_down"], a["wa_up"], a["ba_up"])
        attention(nc, "a1", x_sb, None, shared | {nm[3:]: w[nm] for nm in w if nm.startswith("l1_")}, causal=True)
        channel_mix(nc, x_sb, w, out)


def kernel(**inputs):
    import numpy as np
    import concourse.bacc as _bacc
    from concourse.bass_utils import run_bass_kernel_spmd as _run

    i = {k: np.asarray(v) for k, v in inputs.items()}
    E, HE = 8, 32
    dh = np.arange(P).reshape(H, HD).T.reshape(-1)
    rot = np.arange(P).reshape(H, 2, HD // 2)[:, ::-1].reshape(-1)

    def padded_out(wT, bias=None):
        z = np.zeros((2, 4, 2, 16, P), wT.dtype)
        z[:, :, :, 0:HD] = wT.reshape(2, 4, 2, HD, P)
        if bias is not None:
            z[0, 0, 0, HD] = bias
        return z.reshape(2, P, P).transpose(1, 0, 2)

    w_in, wa = i["L0_attn_w_in"], i["L1_attn_W_attn"]
    arr = {
        "l0_wq": w_in[0:P][dh].T, "l0_wk": w_in[P:2 * P][dh].T, "l0_wv": w_in[2 * P:].T,
        "l0_wo": padded_out(i["L0_attn_w_out"].T, i["L0_attn_b_out"]),
        "l0_bq": i["L0_attn_b_in"][0:P][dh][:, None], "l0_bk": i["L0_attn_b_in"][P:2 * P][dh][:, None],
        "l1_wq": wa[:, 0:P][:, dh], "l1_wqrot": wa[:, 0:P][:, rot][:, dh],
        "l1_wk": wa[:, P:2 * P][:, dh], "l1_wkrot": wa[:, P:2 * P][:, rot][:, dh],
        "l1_wv": wa[:, 2 * P:], "l1_wo": padded_out(i["L1_attn_W_proj"]),
        "w_base": i["L0_ffn_W_base"],
        "wd1": i["L0_ffn_Wd1"].transpose(1, 0, 2).reshape(D, E * HE),
        "wd2": i["L0_ffn_Wd2"].reshape(2, P, D).transpose(1, 0, 2),
        "wd2T": i["L0_ffn_Wd2"].reshape(E * HE, D).T, "bd2T": i["L0_ffn_bd2"].T,
        "w_rT": i["L1_ffn_W_r"].T, "w_kT": i["L1_ffn_W_k"].T, "w_vT": i["L1_ffn_W_v"].T,
        "mu_r": i["L1_ffn_mu_r"][:, None], "mu_k": i["L1_ffn_mu_k"][:, None],
    }
    inv = (1.0 / 10000.0 ** (np.arange(0, HD, 2, dtype=np.float32) / HD)).astype(np.float32)
    freqs = np.arange(T, dtype=np.float32)[:, None] * inv[None, :]
    emb = np.concatenate([freqs, freqs], axis=-1).T
    sign = np.where(np.arange(HD) < HD // 2, -1.0, 1.0)[:, None]
    table = np.stack([np.cos(emb), np.sin(emb) * sign], axis=1).astype(np.float32)
    scale = np.float32(HD ** -0.5)
    rope = np.stack([table * scale, table], axis=1)
    own = np.arange(P)
    row = np.arange(P)[:, None]
    consts = {
        "rope": np.repeat(rope, H, axis=0),
        "ident": np.eye(P), "mask_f": np.where(own[None, :] > own[:, None], -2.0 ** 126, 0.0),
        "den_pick": (row == 16 * np.arange(H // 2)[None, :] + HD) * 1.0, "neghalf": np.full((P, NT), -0.5), "ones": np.ones((P, 1)),
        "block_mask": (row // HE == own[None, :] // HE) * 1.0,
        "expert_of": np.stack([(g * 4 + row // HE == np.arange(E)[None, :]) * 1.0 for g in range(2)], axis=1),
    }
    arr |= {k: v.astype(np.float32) for k, v in consts.items()}
    names = list(arr)
    arr |= {"x": i["L0_attn_x"].reshape(NB * T, D), "l0_bv_row": i["L0_attn_b_in"][None, 2 * P:],
            "bd1_row": i["L0_ffn_bd1"].reshape(1, E * HE), "b_base": i["L0_ffn_b_base"][None, :],
            "wa_down": i["L0_ffn_Wa_down"].reshape(E * D, 64), "ba_down": i["L0_ffn_ba_down"].reshape(E * 64, 1),
            "wa_up": i["L0_ffn_Wa_up"].reshape(E * 64, D), "ba_up": i["L0_ffn_ba_up"]}

    nc = _bacc.Bacc("TRN2", target_bir_lowering=False, num_devices=1)
    arrays, aps = {}, {"_names": names}
    for name, v in arr.items():
        v = np.ascontiguousarray(v)
        arrays[f"in_{name}_dram"] = v
        aps[name] = nc.dram_tensor(f"in_{name}_dram", v.shape, mybir.dt.from_np(v.dtype), kind="ExternalInput").ap()
    out = nc.dram_tensor("out_0_dram", (NB * T, D), F32, kind="ExternalOutput").ap()
    transformer_kernel(nc, aps, out)
    r = _run(nc, [arrays], core_ids=[0])
    return r.results[0]["out_0_dram"].reshape(NB, T, D)
```

```python
import numpy as np
import concourse.bass as bass
from concourse import mybir
from contextlib import ExitStack

F32, BF16, U32 = mybir.dt.float32, mybir.dt.bfloat16, mybir.dt.uint32
ALU, ACT, AX = mybir.AluOpType, mybir.ActivationFunctionType, mybir.AxisListType

NB, T, D = 32, 256, 128
P = 128
NT = T // P
H, HD = 16, 8
NPART = 3
KROWS = NPART * NPART * HD
MROWS = NPART
NBUF = 3
X_FIRST = 4
EPS = 1e-5


class Seq:

    def __init__(self, const, turn=None, per_turn=0):
        self.const, self.turn, self.per_turn = const, turn, per_turn

    def __add__(self, k):
        return Seq(self.const + k, self.turn, self.per_turn)

    def __sub__(self, k):
        return self + -k

    def times(self, n, more=0):
        value = self.const * n + more
        return value if self.turn is None else self.turn * (self.per_turn * n) + value


def live(b):
    return b.turn is not None or 0 <= b.const < NB


def begun(b):
    return b.turn is not None or b.const >= 0


def upto(b, per=1, more=None):
    if b.turn is None and b.const >= NB:
        b, more = Seq(NB - 1), None
    return b.times(per, per if more is None else more)


def upto_in_buffer(b, nbuf, per):
    turns = b.const // nbuf
    return (turns + 1) * per if b.turn is None else b.turn * per + (turns + 1) * per


def run_steps(eng, step, first, last, behind=2, ahead=3, nbuf=NBUF):
    n = (NB - ahead - behind) // nbuf * nbuf
    for s in range(first, behind):
        step(Seq(s), s % nbuf)
    with eng.Fori(0, n // nbuf) as i:
        for k in range(nbuf):
            step(Seq(behind + k, i, nbuf), (behind + k) % nbuf)
    for s in range(behind + n, last + 1):
        step(Seq(s), s % nbuf)


def attention(nc, name, x_sb, loading, w, causal):
    NBUF = 4
    if causal:
        a_chunks = [(0, range(4 * c, 4 * c + 4), P) for c in range(4)]
        a_chunks += [(1, range(2 * c, 2 * c + 2), T) for c in range(8)]
    else:
        a_chunks = [(qt, range(2 * c, 2 * c + 2), T) for qt in range(NT) for c in range(8)]
    b_chunks, group_last = [], []
    for region in range(2):
        for ab in range(2):
            for kt in range(NT):
                if causal and kt == 1:
                    b_chunks.append((region, ab, kt, range(4), P))
                else:
                    b_chunks += [(region, ab, kt, range(2), 0), (region, ab, kt, range(2, 4), 0)]
                group_last.append(len(b_chunks) - 1)
    NA, NBC, NG = len(a_chunks), len(b_chunks), len(group_last)
    NP = 6 if causal else 8
    assert NBC % NP == 0 and NA % 2 == 0 and NBC % 2 == 0
    group_of = [next(g for g in range(NG) if group_last[g] >= c) for c in range(NBC)]
    LATE, PV_LATE = 4, 3
    NPOS = NBC + LATE
    at = [group_last[g] + LATE + PV_LATE for g in range(NG)]
    pv_now = [[g for g in range(NG) if at[g] == p] for p in range(NPOS)]
    pv_before = [[g for g in range(NG) if at[g] == NPOS + p] for p in range(NPOS)]
    TRANSPOSE_X, OUT_1, DEN, INVERT, SPREAD = 1, 3, 4, 5, 6
    RECIP_T, NORMALISE = (9, 9) if causal else (10, 11)
    if causal:
        PROJECT_Q, PROJECT_K, ROPE, ROPE_SUM, PROJECT_V, VALUE = 2, 3, (3, 4), 12, 6, 8
        MOVE_QK, ROUND1, REST1, ROUND2, REST2 = 4, 13, 14, 0, 2
        STATS, RSTD, SPLIT_MAX, OUT_PROJECT, UPDATE, CENTRE = 10, 11, 12, 13, 13, 13
    else:
        PROJECT_Q, PROJECT_K, ROPE, ROPE_SUM, PROJECT_V, VALUE = 3, 3, (4, 4), 5, 5, 6
        MOVE_QK, ROUND1, REST1, ROUND2, REST2 = 3, 12, 13, 0, 1
        STATS, RSTD, SPLIT_MAX, OUT_PROJECT, UPDATE, CENTRE = 13, 15, 16, 17, 18, 17
    OUT_0 = at[NG // 2 - 1] + 1

    scratch = nc.dram_tensor(f"{name}_scratch", (NBUF, 3 * NPART - 1, P, T), BF16).ap()
    ctx = ExitStack()
    with ctx:
        def sb(nm, shape, dt=F32):
            return ctx.enter_context(nc.sbuf_tensor(f"{name}_{nm}", shape, dt))

        def sem(nm):
            return ctx.enter_context(nc.semaphore(f"{name}_{nm}"))

        stats = sb("stats", [P, NBUF, NT, 6])
        meanvar = sb("meanvar", [P, NBUF, NT, 2])
        vareps = sb("vareps", [P, NBUF, NT])
        rstd = sb("rstd", [P, NBUF, NT])
        xn = sb("xn", [P, 2, NT, D])
        xnT = sb("xnT", [P, 2, T])
        qk = sb("qk", [P, 2, 2, T])
        roped = sb("roped", [P, 2, 2, T]) if causal else None
        resid = sb("resid", [P, 2, T])
        parts = sb("parts", [P, 2, 2 * NPART, T], BF16)
        qstack = sb("qstack", [P, NBUF, H * T], BF16)
        kstack = sb("kstack", [P, NBUF, H * T], BF16)
        vpad = sb("vpad", [P, NBUF, NT, H * 32])
        negmax = sb("negmax", [P, NBUF, NT, H])
        mresid = sb("mresid", [P, NT, H])
        mparts = sb("mparts", [P, NBUF, NT, NPART, H], BF16)
        maxT = sb("maxT", [NPART * H, NBUF, T], BF16)
        probs = sb("probs", [P, NP, 2 * T])
        outT = sb("outT", [P, 2, 2 * T])
        recip = sb("recip", [P, 2, NT * H])
        recip16 = sb("recip16", [P, 2 * NT, P])
        outTn = sb("outTn", [P, 2, 2 * T])

        def bank(nm):
            return ctx.enter_context(nc.psum_tensor(f"{name}_{nm}", [P, 512], F32))

        bank_a = [bank("a0"), bank("a1")]
        bank_b = [bank("b0"), bank("b1")]
        bank_o = [bank("o0"), bank("o1")]
        m0, m1 = bank("m0"), bank("m1")
        maxT_ps = m0[0:NPART * H, 0:T // 2].bitcast(BF16)

        stats_done, meanvar_done, vareps_done, rstd_done, xn_done = map(
            sem, ("stats_done", "meanvar_done", "vareps_done", "rstd_done", "xn_done"))
        xnT_in_m0, xnT_ready = sem("xnT_in_m0"), sem("xnT_ready")
        q_in_m1, k_in_m0, qk_moved, qk_ready = sem("q_in_m1"), sem("k_in_m0"), sem("qk_moved"), sem("qk_ready")
        v_in_psum, v_ready = sem("v_in_psum"), sem("v_ready")
        part_rounded, part_taken, parts_ready, stacks_loaded = map(
            sem, ("part_rounded", "part_taken", "parts_ready", "stacks_loaded"))
        a_scored, a_maxed = sem("a_scored"), sem("a_maxed")
        msplit_step, mparts_ready, maxT_in_m0, maxT_ready, maxrow_loaded = map(
            sem, ("msplit_step", "mparts_ready", "maxT_in_m0", "maxT_ready", "maxrow_loaded"))
        b_scored, exp_done, probs_ready = sem("b_scored"), sem("exp_done"), sem("probs_ready")
        if not causal:
            probs_ready = exp_done
        pv_done, out_moved = sem("pv_done"), sem("out_moved")
        recip_spread = sem("recip_spread")
        den_in_o1, recip_done, recip_in_o1, normed = map(sem, ("den_in_o1", "recip_done", "recip_in_o1", "normed"))
        y_in_psum, x_updated = sem("y_in_psum"), sem("x_updated")
        k_ones_set, vpad_set = sem("k_ones_set"), sem("vpad_set")

        def stack_rows(n, which):
            ap = scratch[n, which * NPART, :, :]
            return bass.AP(ap.tensor, ap.offset,
                           [[which * P * T, NPART], [H * T, NPART * HD], [1, H * T]])

        def strided_pairs(pairs):
            ap = pairs[:, :, 0:HD]
            dims = [list(x) for x in ap.ap]
            return bass.AP(ap.tensor, ap.offset, [dims[0], dims[1], [48, 2], dims[2]])

        parts_stored = sem("parts_stored")
        NSTACK = 2
        apart = sem("apart")
        block = ctx.enter_context(nc.Block())

        @block.sync
        def _(sp):
            def step(s, r):
                b, n = s + 2, (r + 2) % NBUF
                if live(b):
                    sp.wait_ge(parts_ready, upto(b))
                    sp.sem_inc(apart, 1)
                    if begun(b - NBUF):
                        sp.wait_ge(b_scored, upto(b - NBUF, NBC))
                        sp.sem_inc(apart, 1)
                    for slot, first, count in ((0, 0, 2 * NPART), (2 * NPART, NPART, NPART - 1)):
                        sp.dma_start(scratch[n, slot:slot + count, :, :].rearrange("a p t -> p a t"),
                                     parts[:, n % 2, first:first + count, :]).then_inc(parts_stored, 16)
                    sp.wait_ge(parts_stored, b.times(32, 32))
                    sp.sem_inc(apart, 1)
                    if b.turn is None and b.const < NBUF:
                        sp.wait_ge(k_ones_set, b.const + 1)
                        sp.sem_inc(apart, 1)
                    if begun(b - 1):
                        sp.wait_ge(stacks_loaded, upto(b - 1, 16 * NSTACK))
                        sp.sem_inc(apart, 1)
                    sp.dma_start(qstack[0:KROWS, n, :], stack_rows(n, 0)).then_inc(stacks_loaded, 16)
                    sp.dma_start(kstack[0:KROWS, n, :], stack_rows(n, 1)).then_inc(stacks_loaded, 16)
                b, n = s + 1, (r + 1) % NBUF
                if live(b):
                    sp.wait_ge(maxT_ready, upto(b))
                    sp.sem_inc(apart, 1)
                    dst = qstack[KROWS:KROWS + MROWS, n, :].rearrange("p (h t) -> p h t", h=H)
                    sp.dma_start(dst, maxT[:, n, :]).then_inc(maxrow_loaded, 16)
            run_steps(sp, step, -3, NB - 2, ahead=4, nbuf=NBUF)
            if loading is not None:
                sp.wait_ge(loading["late"], 16)

        @block.gpsimd
        def _(pool):
            def mask(b, c):
                region, ab, kt, groups, q0 = b_chunks[c]
                pool.wait_ge(exp_done, upto(b, NBC, c + 1))
                pool.sem_inc(apart, 1)
                n = len(groups)
                tile = probs[:, c % NP, :].rearrange("p (g q) -> p g q", g=n)[:, :, 0:P]
                nc.gpsimd.affine_select(out=tile, in_=tile, compare_op=ALU.is_ge, fill=0.0, base=0,
                                        pattern=[[0, n], [1, P]], channel_multiplier=-1)\
                    .then_inc(probs_ready, 1)

            def rest1(s, r):
                b, n = s + 3, (r + 3) % NBUF
                if live(b):
                    if begun(b - 1):
                        pool.wait_ge(parts_ready, upto(b - 1))
                    pool.wait_ge(part_rounded, upto(b, 2, 1))
                    nc.gpsimd.tensor_tensor(resid[:, :, :], qk[:, n % 2, :, :], parts[:, n % 2, 0::NPART, :],
                                            ALU.subtract).then_inc(part_taken, 1)

            def rest2(s, r):
                b, n = s + 2, (r + 2) % NBUF
                if live(b):
                    pool.wait_ge(part_rounded, upto(b, 2))
                    nc.gpsimd.tensor_tensor(parts[:, n % 2, 2::NPART, :], resid[:, :, :],
                                            parts[:, n % 2, 1::NPART, :], ALU.subtract).then_inc(parts_ready, 1)

            def inverse_spread(s, r):
                b, n = s + 4, r
                if live(b):
                    pool.wait_ge(meanvar_done, upto(b, NT))
                    pool.sem_inc(apart, 1)
                    nc.gpsimd.tensor_scalar(vareps[:, n, :], meanvar[:, n, :, 1], EPS, None, ALU.add)\
                        .then_inc(vareps_done, 1)
                    pool.wait_ge(vareps_done, upto(b))
                    pool.sem_inc(apart, 1)
                    nc.gpsimd.tensor_tensor(rstd[:, n, :], vareps[:, n, :], w["neghalf"][:, 0:NT], ALU.pow)\
                        .then_inc(rstd_done, 1)

            def split_max(s, r):
                b, n = s + 1, (r + 1) % NBUF
                if not live(b):
                    return
                pool.wait_ge(a_maxed, upto(b, NA))
                pool.sem_inc(apart, 1)
                m = [mparts[:, n, :, i, :] for i in range(NPART)]
                src = negmax[:, n, :, :]
                nc.gpsimd.tensor_copy(m[0], src).then_inc(msplit_step, 1)
                pool.wait_ge(msplit_step, b.times(3, 1))
                pool.sem_inc(apart, 1)
                nc.gpsimd.tensor_tensor(mresid[:, :, :], src, m[0], ALU.subtract).then_inc(msplit_step, 1)
                pool.wait_ge(msplit_step, b.times(3, 2))
                pool.sem_inc(apart, 1)
                nc.gpsimd.tensor_copy(m[1], mresid[:, :, :]).then_inc(msplit_step, 1)
                pool.wait_ge(msplit_step, b.times(3, 3))
                pool.sem_inc(apart, 1)
                nc.gpsimd.tensor_tensor(m[2], mresid[:, :, :], m[1], ALU.subtract).then_inc(mparts_ready, 1)

            def step(s, r):
                for p in range(NPOS):
                    if p == SPREAD and not causal and live(s - 1):
                        pool.wait_ge(recip_done, upto(s - 1))
                        if begun(s - 2):
                            pool.wait_ge(recip_in_o1, upto(s - 2))
                        ap, one = recip[:, (r - 1) % 2, :], w["ones"][:, :]
                        each16 = bass.AP(ap.tensor, ap.offset, [*[list(x) for x in ap.ap], [0, 16]])
                        ones = bass.AP(one.tensor, one.offset, [list(one.ap[0]), [0, NT * H], [0, 16]])
                        nc.gpsimd.tensor_tensor(recip16[:, :, :].rearrange("p a (h c) -> p (a h) c", c=16), each16,
                                                ones, ALU.mult).then_inc(recip_spread, 1)
                    if p == SPLIT_MAX:
                        split_max(s, r)
                    if causal and p >= LATE and live(s):
                        mask(s, p - LATE)
                    if p == REST1 and not causal:
                        rest1(s, r)
                    if p == REST2 and not causal:
                        rest2(s, r)
                    if p == RSTD:
                        inverse_spread(s, r)
                        if s.turn is None and s.const in (-4, -2):
                            n = (-4, -2).index(s.const)
                            pool.wait_ge(rstd_done, s.const + 5)
                            nc.gpsimd.memset(kstack[64:P, n, :], 1.0).then_inc(k_ones_set, 1)
                            pool.wait_ge(k_ones_set, n + 1)
                if s.turn is None and s.const in (-1, 0):
                    n = s.const + 3
                    pool.wait_ge(mparts_ready, s.const + 2)
                    if causal and s.const == 0:
                        pool.wait_ge(probs_ready, NBC)
                    nc.gpsimd.memset(kstack[64:P, n, :], 1.0).then_inc(k_ones_set, 1)
                    pool.wait_ge(k_ones_set, n + 1)
            run_steps(pool, step, -4, NB, ahead=4, nbuf=NBUF)

        @block.scalar
        def _(act):
            def move_out(b, n, region):
                if live(b):
                    act.wait_ge(pv_done, upto(b, NG, (region + 1) * NG // 2))
                    nc.scalar.activation(outT[:, n % 2, region * T:(region + 1) * T], bank_o[region][:, 0:T],
                                         ACT.Copy).then_inc(out_moved, 1)

            def exponential(s, r, c):
                if live(s):
                    act.wait_ge(b_scored, upto(s, NBC, c + 1))
                    if c >= NP:
                        act.wait_ge(pv_done, upto(s, NG, group_of[c - NP] + 1))
                    else:
                        if begun(s - 1):
                            act.wait_ge(pv_done, upto(s - 1, NG, group_of[c - NP + NBC] + 1))
                    nc.scalar.activation(probs[:, c % NP, :], bank_b[c % 2][:, :], ACT.Exp)\
                        .then_inc(exp_done, 1)

            def step(s, r):
                b, n = s + 3, (r + 3) % NBUF
                for p in range(NPOS):
                    if p == TRANSPOSE_X and live(b):
                        act.wait_ge(xnT_in_m0, upto(b))
                        nc.scalar.activation(xnT[:, n % 2, :], m0[:, 0:T], ACT.Copy).then_inc(xnT_ready, 1)
                    if p == NPOS - 1 and live(s + 1):
                        act.wait_ge(maxT_in_m0, upto(s + 1))
                        nc.scalar.activation(maxT[:, (r + 1) % NBUF, :], maxT_ps, ACT.Copy).then_inc(maxT_ready, 1)
                    if p == OUT_1:
                        move_out(s - 1, (r - 1) % NBUF, 1)
                    if p >= LATE:
                        exponential(s, r, p - LATE)
                    if p == MOVE_QK and live(b) and not causal:
                        act.wait_ge(q_in_m1, upto(b))
                        nc.scalar.activation(qk[:, n % 2, 0, :], m1[:, 0:T], ACT.Identity,
                                             bias=w["bq_scaled"][:, :], scale=float(HD) ** -0.5).then_inc(qk_ready, 1)
                        nc.scalar.activation(qk[:, n % 2, 1, :], m1[:, T:2 * T], ACT.Identity, bias=w["bk"][:, :])\
                            .then_inc(qk_ready, 1)
                    if p == VALUE and live(b) and causal:
                        if b.turn is None and b.const == 0:
                            act.wait_ge(vpad_set, 3)
                        act.wait_ge(v_in_psum, upto(b))
                        for t in range(NT):
                            dst = strided_pairs(vpad[:, n, t, :].rearrange("p (g u) -> p g u", u=64))
                            src = m0[:, t * P:(t + 1) * P].rearrange("p (g a d) -> p g a d", a=2, d=HD)
                            nc.scalar.activation(dst, src, ACT.Copy).then_inc(v_ready, 1)
                    if p == ROUND1 and live(b):
                        act.wait_ge(qk_ready, upto(b, 2))
                        if begun(b - 2):
                            act.wait_ge(parts_stored, upto(b - 2, 32))
                        nc.scalar.activation(parts[:, n % 2, 0::NPART, :], qk[:, n % 2, :, :], ACT.Copy)\
                            .then_inc(part_rounded, 1)
                    if p == ROUND2 and live(s + 2):
                        act.wait_ge(part_taken, upto(s + 2))
                        nc.scalar.activation(parts[:, (r + 2) % 2, 1::NPART, :], resid[:, :, :], ACT.Copy)\
                            .then_inc(part_rounded, 1)
                    if p == SPREAD and causal and live(s - 1):
                        act.wait_ge(recip_done, upto(s - 1))
                        if begun(s - 2):
                            act.wait_ge(recip_in_o1, upto(s - 2))
                        ap = recip[:, (r - 1) % 2, :]
                        each16 = bass.AP(ap.tensor, ap.offset, [*[list(x) for x in ap.ap], [0, 16]])
                        nc.scalar.activation(recip16[:, :, :].rearrange("p a (h c) -> p (a h) c", c=16), each16,
                                             ACT.Copy).then_inc(recip_spread, 1)
                    if p == OUT_0:
                        move_out(s, r, 0)
            run_steps(act, step, -3, NB, ahead=4, nbuf=NBUF)

        @block.vector
        def _(dve):
            def maxima(b, n, c):
                if live(b):
                    qt, heads, keys = a_chunks[c]
                    dve.wait_ge(a_scored, upto(b, NA, c + 1))
                    nc.vector.tensor_reduce(
                        out=negmax[:, n, qt, heads[0]:heads[-1] + 1],
                        in_=bank_a[c % 2][:, :].rearrange("p (h k) -> p h k", k=keys),
                        axis=AX.X, op=ALU.max, negate=True).then_inc(a_maxed, 1)

            def spread(s, r):
                b, n = s + 4, r
                if live(b):
                    if loading is not None and b.turn is None and b.const == X_FIRST:
                        dve.wait_ge(loading["x_rest"], 16)
                    for t in range(NT):
                        nc.vector.bn_stats(stats[:, n, t, :], x_sb[:, bass.ds(b.times(T, t * P), P)])\
                            .then_inc(stats_done, 1)
                    dve.wait_ge(stats_done, upto(b, NT))
                    dve.sem_inc(apart, 1)
                    for t in range(NT):
                        nc.vector.bn_aggr(meanvar[:, n, t, :], stats[:, n, t, :]).then_inc(meanvar_done, 1)

            def centre(s, r):
                b, n = s + 4, r
                if live(b):
                    dve.wait_ge(rstd_done, upto(b))
                    if begun(b - 2):
                        dve.wait_ge(xnT_in_m0, upto(b - 2))
                    for t in range(NT):
                        nc.vector.tensor_scalar(xn[:, n % 2, t, :], x_sb[:, bass.ds(b.times(T, t * P), P)],
                                                meanvar[:, n, t, 0:1], rstd[:, n, t:t + 1],
                                                ALU.subtract, ALU.mult).then_inc(xn_done, 1)

            def rope(s, r, i):
                b = s + 3
                if live(b) and causal:
                    dve.wait_ge((q_in_m1, k_in_m0)[i], upto(b))
                    if begun(b - 1):
                        dve.wait_ge(qk_ready, upto(b - 1, 2))
                    nc.vector.tensor_tensor(roped[:, i, :, :], (m1, m0)[i][:, :].rearrange("p (a t) -> p a t", a=2),
                                            w["rope"][:, i, :, :], ALU.mult).then_inc(qk_moved, 1)

            def rope_sum(s, r):
                b, n = s + 3, (r + 3) % NBUF
                if live(b) and causal:
                    dve.wait_ge(qk_moved, upto(b, 2))
                    nc.vector.tensor_tensor(qk[:, n % 2, :, :], roped[:, :, 0, :], roped[:, :, 1, :], ALU.add)\
                        .then_inc(qk_ready, 2)

            def rest1(s, r):
                b, n = s + 3, (r + 3) % NBUF
                if live(b):
                    if begun(b - 1):
                        dve.wait_ge(parts_ready, upto(b - 1))
                    dve.wait_ge(part_rounded, upto(b, 2, 1))
                    nc.vector.tensor_tensor(resid[:, :, :], qk[:, n % 2, :, :], parts[:, n % 2, 0::NPART, :],
                                            ALU.subtract).then_inc(part_taken, 1)

            def rest2(s, r):
                b, n = s + 2, (r + 2) % NBUF
                if live(b):
                    dve.wait_ge(part_rounded, upto(b, 2))
                    nc.vector.tensor_tensor(parts[:, n % 2, 2::NPART, :], resid[:, :, :],
                                            parts[:, n % 2, 1::NPART, :], ALU.subtract).then_inc(parts_ready, 1)

            def value(s, r):
                b, n = s + 3, (r + 3) % NBUF
                if live(b) and not causal:
                    if b.turn is None and b.const == 0:
                        dve.wait_ge(vpad_set, 3)
                    dve.wait_ge(v_in_psum, upto(b))
                    for t in range(NT):
                        dst = strided_pairs(vpad[:, n, t, :].rearrange("p (g u) -> p g u", u=64))
                        src = m0[:, t * P:(t + 1) * P].rearrange("p (g a d) -> p g a d", a=2, d=HD)
                        bias = w["bv"][:, :].rearrange("p (g a d) -> p g a d", a=2, d=HD)
                        nc.vector.tensor_tensor(dst, src, bias, ALU.add).then_inc(v_ready, 1)

            def invert(s, r):
                b, n = s - 1, (r - 1) % NBUF
                if live(b):
                    dve.wait_ge(den_in_o1, upto(b))
                    nc.vector.reciprocal(recip[:, n % 2, :], bank_o[1][:, 0:NT * H]).then_inc(recip_done, 1)

            def normalise(s, r):
                b, n = s - 1, (r - 1) % NBUF
                if live(b):
                    dve.wait_ge(recip_in_o1, upto(b))
                    nc.vector.tensor_tensor(outTn[:, n % 2, :], bank_o[1][:, :], outT[:, n % 2, :], ALU.mult)\
                        .then_inc(normed, 1)

            def update(s, r):
                b = s - 1
                if live(b):
                    dve.wait_ge(y_in_psum, upto(b))
                    tile = x_sb[:, bass.ds(b.times(T), T)]
                    nc.vector.tensor_tensor(tile, m1[:, 0:T], tile, ALU.add).then_inc(x_updated, 1)

            def step(s, r):
                for p in range(NPOS):
                    for i in range(2):
                        if causal and p == ROPE[i]:
                            rope(s, r, i)
                    if p == INVERT:
                        invert(s, r)
                    if p < NA:
                        maxima(s + 1, (r + 1) % NBUF, p)
                    if p == VALUE:
                        value(s, r)
                    if p == NORMALISE:
                        normalise(s, r)
                    if p == ROPE_SUM:
                        rope_sum(s, r)
                    if p == UPDATE:
                        update(s, r)
                    if p == REST1 and causal:
                        rest1(s, r)
                    if p == REST2 and causal:
                        rest2(s, r)
                    if p == STATS:
                        spread(s, r)
                    if p == CENTRE:
                        centre(s, r)
                if s.turn is None and s.const == -4:
                    pairs = vpad[:, :, :, :].rearrange("p n t (g u) -> p (n t) g u", u=64)
                    nc.vector.memset(vpad[:, :, :, :], 0.0).then_inc(vpad_set, 1)
                    dve.wait_ge(vpad_set, 1)
                    nc.vector.memset(pairs[:, :, :, 8:16], 1.0).then_inc(vpad_set, 1)
                    nc.vector.memset(pairs[:, :, :, 56:64], 1.0).then_inc(vpad_set, 1)
            if loading is not None:
                dve.wait_ge(loading["x_first"], 16)
            run_steps(dve, step, -4, NB, ahead=4, nbuf=NBUF)

        @block.tensor
        def _(pe):
            def score_a(b, n, c):
                if not live(b):
                    return
                if c == 0:
                    pe.wait_ge(stacks_loaded, upto(b, 16 * NSTACK))
                qt, heads, keys = a_chunks[c]
                if c >= 2:
                    pe.wait_ge(a_maxed, upto(b, NA, c - 1))
                else:
                    if begun(b - 1):
                        pe.wait_ge(a_maxed, upto(b - 1, NA, NA + c - 1))
                ps = bank_a[c % 2]
                if causal:
                    masked = ps[:, :].rearrange("p (h k) -> p h k", k=keys)[:, :, keys - P:keys]
                    nc.tensor.matmul(masked, w["ident_bf"][:, :], w["mask"][:, 0:len(heads), :],
                                     start=True, stop=False, skip_group_check=True)
                for i, h in enumerate(heads):
                    last = nc.tensor.matmul(
                        ps[:, i * keys:(i + 1) * keys],
                        qstack[0:KROWS, n, h * T + qt * P:h * T + qt * P + P],
                        kstack[0:KROWS, n, h * T:h * T + keys],
                        start=not causal, stop=True, skip_group_check=causal)
                last.then_inc(a_scored, 1)

            def score_b(b, n, c):
                if not live(b):
                    return
                if c == 0:
                    pe.wait_ge(maxrow_loaded, upto(b, 16))
                region, ab, kt, groups, q0 = b_chunks[c]
                if c >= 2:
                    pe.wait_ge(exp_done, upto(b, NBC, c - 1))
                else:
                    if begun(b - 1):
                        pe.wait_ge(exp_done, upto(b - 1, NBC, NBC + c - 1))
                nq = T - q0
                for i, j in enumerate(groups):
                    h = region * 8 + j * 2 + ab
                    last = nc.tensor.matmul(
                        bank_b[c % 2][:, i * nq:(i + 1) * nq],
                        kstack[0:KROWS + MROWS, n, h * T + kt * P:h * T + kt * P + P],
                        qstack[0:KROWS + MROWS, n, h * T + q0:(h + 1) * T], start=True, stop=True)
                last.then_inc(b_scored, 1)

            def weigh(b, n, g):
                if not live(b):
                    return
                if g == 0:
                    pe.wait_ge(v_ready, upto(b, NT))
                region, ab, kt, groups, q0 = b_chunks[group_last[g]]
                if g % (NG // 2) == 0:
                    if begun(b - 1):
                        pe.wait_ge(out_moved, upto(b - 1, 2, region + 1))
                    if region == 1 and begun(b - 1):
                        pe.wait_ge(normed, upto(b - 1))
                pe.wait_ge(probs_ready, upto(b, NBC, group_last[g] + 1))
                nq = T - q0
                for j in range(4):
                    h = region * 8 + j * 2 + ab
                    c = next(c for c in range(NBC) if b_chunks[c][:3] == (region, ab, kt) and j in b_chunks[c][3])
                    i = j - b_chunks[c][3][0]
                    last = nc.tensor.matmul(
                        bank_o[region][32 * j:32 * j + 32, q0:T],
                        vpad[:, n, kt, h * 32:(h + 1) * 32],
                        probs[:, c % NP, i * nq:(i + 1) * nq],
                        start=(g % (NG // 2) == 0), stop=(g % (NG // 2) == NG // 2 - 1))
                last.then_inc(pv_done, 1)

            def transpose_x(s, r):
                b, n = s + 3, (r + 3) % NBUF
                if live(b):
                    pe.wait_ge(xn_done, upto(b, NT))
                    if begun(b - 1):
                        pe.wait_ge(v_ready, upto(b - 1, NT))
                    if begun(s):
                        pe.wait_ge(maxT_ready, upto(s))
                    for t in range(NT):
                        last = nc.tensor.transpose(m0[:, t * P:(t + 1) * P], xn[:, n % 2, t, :], w["ident"][:, :])
                    last.then_inc(xnT_in_m0, 1)

            def project_q(s, r):
                b, n = s + 3, (r + 3) % NBUF
                if live(b):
                    pe.wait_ge(xnT_ready, upto(b))
                    if begun(s - 2):
                        pe.wait_ge(x_updated, upto(s - 2))
                    nc.tensor.matmul(m1[:, 0:T], w["wq"][:, :], xnT[:, n % 2, :], start=True, stop=True)
                    nc.tensor.matmul(m1[:, T:2 * T], w["wqrot" if causal else "wk"][:, :], xnT[:, n % 2, :],
                                     start=True, stop=True).then_inc(q_in_m1, 1)

            def project_k(s, r):
                b, n = s + 3, (r + 3) % NBUF
                if live(b) and causal:
                    nc.tensor.matmul(m0[:, 0:T], w["wk"][:, :], xnT[:, n % 2, :], start=True, stop=True)
                    nc.tensor.matmul(m0[:, T:2 * T], w["wkrot"][:, :], xnT[:, n % 2, :],
                                     start=True, stop=True).then_inc(k_in_m0, 1)

            def project_v(s, r):
                b, n = s + 3, (r + 3) % NBUF
                if live(b):
                    if causal:
                        pe.wait_ge(qk_moved, upto(b, 2))
                    for t in range(NT):
                        last = nc.tensor.matmul(m0[:, t * P:(t + 1) * P], xnT[:, n % 2, t * P:(t + 1) * P],
                                                w["wv"][:, :], start=True, stop=True)
                    last.then_inc(v_in_psum, 1)

            def pick_den(s, r):
                b, n = s - 1, (r - 1) % NBUF
                if live(b):
                    pe.wait_ge(out_moved, upto(b, 2))
                    for t in range(NT):
                        for region in range(2):
                            at = (t * 2 + region) * H // 2
                            last = nc.tensor.matmul(bank_o[1][:, at:at + H // 2],
                                                    outT[:, n % 2, region * T + t * P:region * T + (t + 1) * P],
                                                    w["den_pick"][:, :], start=True, stop=True)
                    last.then_inc(den_in_o1, 1)

            def spread_recip(s, r):
                b, n = s - 1, (r - 1) % NBUF
                if live(b):
                    pe.wait_ge(recip_spread, upto(b))
                    for t in range(NT):
                        for region in range(2):
                            last = nc.tensor.transpose(bank_o[1][:, region * T + t * P:region * T + (t + 1) * P],
                                                       recip16[:, t * 2 + region, :], w["ident"][:, :])
                    last.then_inc(recip_in_o1, 1)

            def project_out(s, r):
                b, n = s - 1, (r - 1) % NBUF
                if live(b):
                    pe.wait_ge(normed, upto(b))
                    pe.wait_ge(qk_moved if causal else qk_ready, upto(s + 3, 2))
                    for t in range(NT):
                        for region in range(2):
                            last = nc.tensor.matmul(
                                m1[:, t * P:(t + 1) * P],
                                outTn[:, n % 2, region * T + t * P:region * T + (t + 1) * P],
                                w["wo"][:, region, :], start=(region == 0), stop=(region == 1))
                    last.then_inc(y_in_psum, 1)

            def transpose_max(s, r):
                b, n = s + 1, (r + 1) % NBUF
                if live(b):
                    pe.wait_ge(v_ready, upto(s + 3, NT))
                    pe.wait_ge(mparts_ready, upto(b))
                    pe.sem_inc(apart, 1)
                    for t in range(NT):
                        last = nc.tensor.transpose(
                            maxT_ps[:, t * P:(t + 1) * P],
                            mparts[:, n, t, :, :].rearrange("p a h -> p (a h)"), w["ident_bf"][:, :])
                    last.then_inc(maxT_in_m0, 1)

            def step(s, r):
                for p in range(NPOS):
                    if p == TRANSPOSE_X:
                        transpose_x(s, r)
                    if p == PROJECT_Q:
                        project_q(s, r)
                    if p == PROJECT_K:
                        project_k(s, r)
                    if p == PROJECT_V:
                        project_v(s, r)
                    if p == DEN:
                        pick_den(s, r)
                    if p == RECIP_T:
                        spread_recip(s, r)
                    if p == OUT_PROJECT:
                        project_out(s, r)
                    if p == NPOS - 1:
                        transpose_max(s, r)
                    if p < NA:
                        score_a(s + 1, (r + 1) % NBUF, p)
                    if p >= LATE:
                        score_b(s, r, p - LATE)
                    for g in pv_before[p]:
                        weigh(s - 1, (r - 1) % NBUF, g)
                    for g in pv_now[p]:
                        weigh(s, r, g)
            run_steps(pe, step, -3, NB, ahead=4, nbuf=NBUF)


def expert_ffn(nc, x_sb, w, wa_down, ba_down, wa_up, ba_up):
    NBF = 6
    E, HE, R = 8, 32, 64
    XC, OC, H1C, HXW = P, 2 * P, 2 * P + 1, 3 * P + 1
    MC = 2 * P + 1
    ctx = ExitStack()
    with ctx:
        def sb(nm, shape, dt=F32):
            return ctx.enter_context(nc.sbuf_tensor(f"f0_{nm}", shape, dt))

        def sem(nm):
            return ctx.enter_context(nc.semaphore(f"f0_{nm}"))

        stats = sb("stats", [P, NBF, NT, 6])
        meanvar = sb("meanvar", [P, NBF, NT, 2])
        vareps = sb("vareps", [P, NBF, NT])
        rstd = sb("rstd", [P, NBF, NT])
        hx = sb("hx", [P, NBF, NT, HXW])
        xnT = sb("xnT", [P, NBF, T])
        xsum = sb("xsum", [P, NBF])
        hpre = sb("hpre", [P, NBF, NT, 2 * P])
        weighed = sb("weighed", [P, NBF, 2, MC])
        rowloss = sb("rowloss", [P, NBF, 2])
        negloss = sb("negloss", [1, NBF, E])
        best8 = sb("best8", [1, NBF, 8])
        best_at = sb("best_at", [1, NBF, 8], U32)
        wd_sel = sb("wd_sel", [P, NBF, R])
        bd_sel = sb("bd_sel", [R, NBF, 1])
        wu_sel = sb("wu_sel", [R + 2, NBF, D])
        hidT = sb("hidT", [R + 2, NBF, T])

        def bank(nm):
            return ctx.enter_context(nc.psum_tensor(f"f0_{nm}", [P, 512], F32))

        ps_x, ps_h, ps_g, ps_l, ps_d, ps_y = (bank("x"), bank("h"), [bank("g0"), bank("g1")], bank("l"),
                                             bank("d"), bank("y"))
        stats_done, meanvar_done, vareps_done, rstd_done, xn_done = map(
            sem, ("stats_done", "meanvar_done", "vareps_done", "rstd_done", "xn_done"))
        xnT_in_psum, xnT_ready, h_in_psum, h_biased, h_ready = map(
            sem, ("xnT_in_psum", "xnT_ready", "h_in_psum", "h_biased", "h_ready"))
        moments_in_psum, moments_weighed, loss_in_psum, loss_moved, best_found, expert_known = map(
            sem, ("moments_in_psum", "moments_weighed", "loss_in_psum", "loss_moved", "best_found",
                  "expert_known"))
        down_in_psum, hid_ready, y_in_psum, x_updated, consts_set = map(
            sem, ("down_in_psum", "hid_ready", "y_in_psum", "x_updated", "consts_set"))
        adapter_loaded = [sem(f"adapter_loaded{n}") for n in range(NBF)]
        base_loaded, apart = sem("base_loaded"), sem("apart")
        NCONST = 2
        block = ctx.enter_context(nc.Block())

        def steps(eng, step, first, last):
            run_steps(eng, step, first, last, behind=6, ahead=3, nbuf=NBF)

        @block.sync
        def _(sp):
            for n in range(NBF):
                sp.dma_start(wu_sel[R + 1:R + 2, n, :], w["b_base_dram"]).then_inc(base_loaded, 16)
            sp.wait_ge(base_loaded, 16 * NBF)

            def step(s, n):
                if not live(s):
                    return
                sp.wait_ge(expert_known, upto(s))
                sp.sem_inc(apart, 1)
                if begun(s - NBF):
                    sp.wait_ge(y_in_psum, upto(s - NBF))
                    sp.sem_inc(apart, 1)
                e = sp.value_load(best_at[0:1, n, 0:1], min_val=0, max_val=E - 1)
                sp.dma_start(wd_sel[:, n, :], wa_down[bass.ds(e * D, D), :]).then_inc(adapter_loaded[n], 16)
                sp.dma_start(bd_sel[:, n, :], ba_down[bass.ds(e * R, R), :]).then_inc(adapter_loaded[n], 16)
                sp.dma_start(wu_sel[0:R, n, :], wa_up[bass.ds(e * R, R), :]).then_inc(adapter_loaded[n], 16)
                sp.dma_start(wu_sel[R:R + 1, n, :], ba_up[bass.ds(e, 1), :]).then_inc(adapter_loaded[n], 16)
            steps(sp, step, 0, NB - 1)

        @block.gpsimd
        def _(pool):
            nc.gpsimd.memset(hx[:, :, :, OC:OC + 1], 1.0).then_inc(consts_set, 1)
            pool.wait_ge(consts_set, 1)
            nc.gpsimd.memset(hidT[R:R + 2, :, :], 1.0).then_inc(consts_set, 1)

            def step(s, n):
                b, n = s + 3, (n + 3) % NBF
                if live(b):
                    pool.wait_ge(meanvar_done, upto(b, NT))
                    pool.sem_inc(apart, 1)
                    nc.gpsimd.tensor_scalar(vareps[:, n, :], meanvar[:, n, :, 1], EPS, None, ALU.add)\
                        .then_inc(vareps_done, 1)
                    pool.wait_ge(vareps_done, upto(b))
                    nc.gpsimd.tensor_tensor(rstd[:, n, :], vareps[:, n, :], w["neghalf"][:, 0:NT], ALU.pow)\
                        .then_inc(rstd_done, 1)
            steps(pool, step, -3, NB - 4)

        @block.scalar
        def _(act):
            def step(s, r):
                b, n = s + 1, (r + 1) % NBF
                if live(b):
                    act.wait_ge(xnT_in_psum, upto(b))
                    nc.scalar.activation(xnT[:, n, :], ps_x[:, 0:T], ACT.Copy, accum_out=xsum[:, n:n + 1])\
                        .then_inc(xnT_ready, 1)
                b, n = s - 3, (r - 3) % NBF
                if live(b):
                    act.wait_ge(down_in_psum, upto(b))
                    nc.scalar.activation(hidT[0:R, n, :], ps_d[0:R, 0:T], ACT.Relu, bias=bd_sel[:, n, :])\
                        .then_inc(hid_ready, 1)
                b, n = s + 1, (r + 1) % NBF
                if live(b):
                    act.wait_ge(h_biased, upto(b))
                    if begun(b - NBF):
                        act.wait_ge(moments_in_psum, upto(b - NBF, 2))
                    for t in range(NT):
                        ap = hx[:, n, t, 0:P]
                        dims = [list(x) for x in ap.ap]
                        dst = bass.AP(ap.tensor, ap.offset, [dims[0], [H1C, 2], dims[1]])
                        nc.scalar.activation(dst, hpre[:, n, t, :].rearrange("p (g h) -> p g h", g=2),
                                             ACT.Relu).then_inc(h_ready, 1)
            act.wait_ge(consts_set, NCONST)
            steps(act, step, -1, NB + 2)

        @block.vector
        def _(dve):
            def norm(s, r):
                b, n = s + 3, (r + 3) % NBF
                if live(b):
                    for t in range(NT):
                        nc.vector.bn_stats(stats[:, n, t, :], x_sb[:, bass.ds(b.times(T, t * P), P)])\
                            .then_inc(stats_done, 1)
                    dve.wait_ge(stats_done, upto(b, NT))
                    dve.sem_inc(apart, 1)
                    for t in range(NT):
                        nc.vector.bn_aggr(meanvar[:, n, t, :], stats[:, n, t, :]).then_inc(meanvar_done, 1)

            def centre(s, r):
                b, n = s + 2, (r + 2) % NBF
                if live(b):
                    dve.wait_ge(rstd_done, upto(b))
                    if begun(b - NBF):
                        dve.wait_ge(moments_in_psum, upto(b - NBF, 2))
                    for t in range(NT):
                        nc.vector.tensor_scalar(hx[:, n, t, XC:XC + D], x_sb[:, bass.ds(b.times(T, t * P), P)],
                                                meanvar[:, n, t, 0:1], rstd[:, n, t:t + 1],
                                                ALU.subtract, ALU.mult).then_inc(xn_done, 1)

            def step(s, r):
                centre(s, r)
                if live(s):
                    dve.wait_ge(moments_in_psum, upto(s, 2))
                    for g in range(2):
                        nc.vector.tensor_tensor_reduce(
                            out=weighed[:, r, g, :], in0=ps_g[g][:, 0:MC], in1=w["moment_weights"][:, g, :],
                            scale=1.0, scalar=0.0, op0=ALU.mult, op1=ALU.add,
                            accum_out=rowloss[:, r, g:g + 1]).then_inc(moments_weighed, 1)
                b, n = s + 1, (r + 1) % NBF
                if live(b):
                    dve.wait_ge(h_in_psum, upto(b))
                    nc.vector.tensor_tensor(hpre[:, n, :, :], ps_h[:, :].rearrange("p (t h) -> p t h", t=NT),
                                            w["bd1"][:, :, :], ALU.add).then_inc(h_biased, 1)
                norm(s, r)
                if live(s):
                    dve.wait_ge(loss_in_psum, upto(s))
                    nc.vector.tensor_copy(negloss[:, r, :], ps_l[0:1, 0:E]).then_inc(loss_moved, 1)
                    dve.wait_ge(loss_moved, upto(s))
                    dve.sem_inc(apart, 1)
                    nc.vector.max(best8[:, r, :], negloss[:, r, :]).then_inc(best_found, 1)
                    dve.wait_ge(best_found, upto(s))
                    dve.sem_inc(apart, 1)
                    nc.vector.max_index(best_at[:, r, :], best8[:, r, :], negloss[:, r, :])\
                        .then_inc(expert_known, 1)
                b = s - 3
                if live(b):
                    dve.wait_ge(y_in_psum, upto(b))
                    tile = x_sb[:, bass.ds(b.times(T), T)]
                    nc.vector.tensor_tensor(tile, ps_y[:, 0:T], tile, ALU.add).then_inc(x_updated, 1)
            dve.wait_ge(consts_set, NCONST)
            steps(dve, step, -3, NB + 2)

        @block.tensor
        def _(pe):
            def step(s, r):
                b, n = s + 1, (r + 1) % NBF
                if live(b):
                    pe.wait_ge(xn_done, upto(b, NT))
                    if begun(b - 1):
                        pe.wait_ge(xnT_ready, upto(b - 1))
                    for t in range(NT):
                        last = nc.tensor.transpose(ps_x[:, t * P:(t + 1) * P], hx[:, n, t, XC:XC + D],
                                                   w["ident"][:, :])
                    last.then_inc(xnT_in_psum, 1)
                b, m = s - 3, (r - 3) % NBF
                if live(b):
                    pe.wait_ge(adapter_loaded[m], upto_in_buffer(b, NBF, 64))
                    if begun(b - 1):
                        pe.wait_ge(hid_ready, upto(b - 1))
                    nc.tensor.matmul(ps_d[0:R, 0:T], wd_sel[:, m, :], xnT[:, m, :], start=True, stop=True)\
                        .then_inc(down_in_psum, 1)
                if live(s):
                    pe.wait_ge(h_ready, upto(s, NT))
                    if begun(s - 1):
                        pe.wait_ge(moments_weighed, upto(s - 1, 2))
                    for g in range(2):
                        for t in range(NT):
                            last = nc.tensor.matmul(
                                ps_g[g][:, 0:MC], hx[:, r, t, g * H1C:g * H1C + P],
                                hx[:, r, t, g * P:g * P + MC], start=(t == 0), stop=(t == NT - 1))
                        last.then_inc(moments_in_psum, 1)
                if live(s + 1):
                    pe.wait_ge(xnT_ready, upto(s + 1))
                    pe.wait_ge(h_biased, upto(s))
                    for t in range(NT):
                        last = nc.tensor.matmul(ps_h[:, t * 2 * P:(t + 1) * 2 * P],
                                                xnT[:, n, t * P:(t + 1) * P], w["wd1"][:, :],
                                                start=True, stop=True)
                    last.then_inc(h_in_psum, 1)
                if live(b):
                    pe.wait_ge(hid_ready, upto(b))
                    if begun(b - 1):
                        pe.wait_ge(x_updated, upto(b - 1))
                    for t in range(NT):
                        nc.tensor.matmul(ps_y[:, t * P:(t + 1) * P], xnT[:, m, t * P:(t + 1) * P],
                                         w["w_base"][:, :], start=True, stop=False)
                        last = nc.tensor.matmul(ps_y[:, t * P:(t + 1) * P], hidT[:, m, t * P:(t + 1) * P],
                                                wu_sel[:, m, :], start=False, stop=True)
                    last.then_inc(y_in_psum, 1)
                if live(s):
                    pe.wait_ge(moments_weighed, upto(s, 2))
                    if begun(s - 1):
                        pe.wait_ge(loss_moved, upto(s - 1))
                    for g in range(2):
                        nc.tensor.matmul(ps_l[0:1, 0:E], rowloss[:, r, g:g + 1], w["neg_expert"][:, g, :],
                                         start=(g == 0), stop=False)
                    nc.tensor.matmul(ps_l[0:1, 0:E], xsum[:, r:r + 1], w["twice_bd2T"][:, :],
                                     start=False, stop=False)
                    nc.tensor.matmul(ps_l[0:1, 0:E], w["ones"][0:1, 0:1], w["neg_bias_loss"][:, :],
                                     start=False, stop=True).then_inc(loss_in_psum, 1)
            pe.wait_ge(consts_set, NCONST)
            steps(pe, step, -1, NB + 2)


def channel_mix(nc, x_sb, w, out):
    ctx = ExitStack()
    with ctx:
        def sb(nm, shape, dt=F32):
            return ctx.enter_context(nc.sbuf_tensor(f"f1_{nm}", shape, dt))

        def sem(nm):
            return ctx.enter_context(nc.semaphore(f"f1_{nm}"))

        def bank(nm):
            return ctx.enter_context(nc.psum_tensor(f"f1_{nm}", [P, 512], F32))

        stats = sb("stats", [P, NBUF, NT, 6])
        meanvar = sb("meanvar", [P, NBUF, NT, 2])
        vareps = sb("vareps", [P, NBUF, NT])
        rstd = sb("rstd", [P, NBUF, NT])
        xn = sb("xn", [P, NBUF, NT, D])
        xnT = sb("xnT", [P, NBUF, 1 + T])
        delta = sb("delta", [P, NBUF, T])
        mixed = sb("mixed", [P, NBUF, 2, T])
        tanh_r = sb("tanh_r", [P, NBUF, T])
        relu_k = sb("relu_k", [P, NBUF, T])
        k_act = sb("k_act", [P, NBUF, T])
        gated = sb("gated", [P, NBUF, T])
        ps_x, ps_r, ps_k, ps_v = bank("x"), bank("r"), bank("k"), bank("v")
        stats_done, meanvar_done, vareps_done, rstd_done, xn_done = map(
            sem, ("stats_done", "meanvar_done", "vareps_done", "rstd_done", "xn_done"))
        xnT_in_psum, xnT_ready, delta_ready, mixed_ready = map(
            sem, ("xnT_in_psum", "xnT_ready", "delta_ready", "mixed_ready"))
        r_in_psum, tanh_ready, k_in_psum, relu_ready, k_ready = map(
            sem, ("r_in_psum", "tanh_ready", "k_in_psum", "relu_ready", "k_ready"))
        v_in_psum, gated_ready, result_ready, stored, consts_set = map(
            sem, ("v_in_psum", "gated_ready", "result_ready", "stored", "consts_set"))
        apart = sem("apart")
        out_v = out.rearrange("(n p) d -> p n d", p=P)
        block = ctx.enter_context(nc.Block())

        def steps(eng, step, first, last):
            run_steps(eng, step, first, last, behind=2, ahead=2)

        @block.sync
        def _(sp):
            def step(s, r):
                b = s - 1
                if live(b):
                    sp.wait_ge(result_ready, upto(b))
                    sp.sem_inc(apart, 1)
                    src = x_sb[:, bass.ds(b.times(T), T)].rearrange("p (t d) -> p t d", t=NT)
                    sp.dma_start(out_v[:, bass.ds(b.times(NT), NT), :], src).then_inc(stored, 16)
            steps(sp, step, 1, NB)
            sp.wait_ge(stored, 16 * NB)

        @block.gpsimd
        def _(pool):
            nc.gpsimd.memset(xnT[:, :, 0:1], 0.0).then_inc(consts_set, 1)

            def step(s, r):
                b, n = s + 1, (r + 1) % NBUF
                if live(b):
                    pool.wait_ge(xnT_ready, upto(b))
                    nc.gpsimd.tensor_tensor(delta[:, n, :], xnT[:, n, 1:1 + T], xnT[:, n, 0:T], ALU.subtract)\
                        .then_inc(delta_ready, 1)
                b, n = s + 2, (r + 2) % NBUF
                if live(b):
                    pool.wait_ge(meanvar_done, upto(b, NT))
                    pool.sem_inc(apart, 1)
                    nc.gpsimd.tensor_scalar(vareps[:, n, :], meanvar[:, n, :, 1], EPS, None, ALU.add)\
                        .then_inc(vareps_done, 1)
                    pool.wait_ge(vareps_done, upto(b))
                    nc.gpsimd.tensor_tensor(rstd[:, n, :], vareps[:, n, :], w["neghalf"][:, 0:NT], ALU.pow)\
                        .then_inc(rstd_done, 1)
            steps(pool, step, -2, NB)

        @block.scalar
        def _(act):
            def step(s, r):
                b, n = s + 1, (r + 1) % NBUF
                if live(b):
                    act.wait_ge(xnT_in_psum, upto(b))
                    nc.scalar.activation(xnT[:, n, 1:1 + T], ps_x[:, 0:T], ACT.Copy).then_inc(xnT_ready, 1)
                if live(s):
                    act.wait_ge(k_in_psum, upto(s))
                    nc.scalar.activation(relu_k[:, r, :], ps_k[:, 0:T], ACT.Relu).then_inc(relu_ready, 1)
                    act.wait_ge(r_in_psum, upto(s))
                    nc.scalar.activation(tanh_r[:, r, :], ps_r[:, 0:T], ACT.Tanh, scale=0.5)\
                        .then_inc(tanh_ready, 1)
                    act.wait_ge(relu_ready, upto(s))
                    nc.scalar.activation(k_act[:, r, :], relu_k[:, r, :], ACT.Square).then_inc(k_ready, 1)
            act.wait_ge(consts_set, 1)
            steps(act, step, -1, NB)

        @block.vector
        def _(dve):
            def step(s, r):
                b, n = s + 2, (r + 2) % NBUF
                if live(b):
                    for t in range(NT):
                        nc.vector.bn_stats(stats[:, n, t, :], x_sb[:, bass.ds(b.times(T, t * P), P)])\
                            .then_inc(stats_done, 1)
                    dve.wait_ge(stats_done, upto(b, NT))
                    dve.sem_inc(apart, 1)
                    for t in range(NT):
                        nc.vector.bn_aggr(meanvar[:, n, t, :], stats[:, n, t, :]).then_inc(meanvar_done, 1)
                b, n = s - 1, (r - 1) % NBUF
                if live(b):
                    dve.wait_ge(v_in_psum, upto(b))
                    nc.vector.scalar_tensor_tensor(out=gated[:, n, :], in0=tanh_r[:, n, :], scalar=1.0,
                                                   in1=ps_v[:, 0:T], op0=ALU.add, op1=ALU.mult)\
                        .then_inc(gated_ready, 1)
                b, n = s + 1, (r + 1) % NBUF
                if live(b):
                    dve.wait_ge(delta_ready, upto(b))
                    for i, mu in enumerate(("mu_r", "mu_k")):
                        nc.vector.scalar_tensor_tensor(out=mixed[:, n, i, :], in0=delta[:, n, :],
                                                       scalar=w[mu][:, :], in1=xnT[:, n, 0:T],
                                                       op0=ALU.mult, op1=ALU.add).then_inc(mixed_ready, 1)
                b, n = s + 2, (r + 2) % NBUF
                if live(b):
                    dve.wait_ge(rstd_done, upto(b))
                    for t in range(NT):
                        nc.vector.tensor_scalar(xn[:, n, t, :], x_sb[:, bass.ds(b.times(T, t * P), P)],
                                                meanvar[:, n, t, 0:1], rstd[:, n, t:t + 1],
                                                ALU.subtract, ALU.mult).then_inc(xn_done, 1)
                b, n = s - 1, (r - 1) % NBUF
                if live(b):
                    dve.wait_ge(gated_ready, upto(b))
                    tile = x_sb[:, bass.ds(b.times(T), T)]
                    nc.vector.scalar_tensor_tensor(out=tile, in0=gated[:, n, :], scalar=0.5, in1=tile,
                                                   op0=ALU.mult, op1=ALU.add).then_inc(result_ready, 1)
            steps(dve, step, -2, NB)

        @block.tensor
        def _(pe):
            def step(s, r):
                b, n = s + 1, (r + 1) % NBUF
                if live(b):
                    pe.wait_ge(xn_done, upto(b, NT))
                    if begun(b - 1):
                        pe.wait_ge(xnT_ready, upto(b - 1))
                    for t in range(NT):
                        last = nc.tensor.transpose(ps_x[:, t * P:(t + 1) * P], xn[:, n, t, :], w["ident"][:, :])
                    last.then_inc(xnT_in_psum, 1)
                b, n = s - 1, (r - 1) % NBUF
                if live(b):
                    pe.wait_ge(k_ready, upto(b))
                    if begun(b - 1):
                        pe.wait_ge(gated_ready, upto(b - 1))
                    for t in range(NT):
                        last = nc.tensor.matmul(ps_v[:, t * P:(t + 1) * P], k_act[:, n, t * P:(t + 1) * P],
                                                w["w_vT"][:, :], start=True, stop=True)
                    last.then_inc(v_in_psum, 1)
                if live(s):
                    pe.wait_ge(mixed_ready, upto(s, 2))
                    if begun(s - 1):
                        pe.wait_ge(relu_ready, upto(s - 1))
                    nc.tensor.matmul(ps_k[:, 0:T], w["w_kT"][:, :], mixed[:, r, 1, :], start=True, stop=True)\
                        .then_inc(k_in_psum, 1)
                    if begun(s - 1):
                        pe.wait_ge(tanh_ready, upto(s - 1))
                    for t in range(NT):
                        last = nc.tensor.matmul(ps_r[:, t * P:(t + 1) * P], mixed[:, r, 0, t * P:(t + 1) * P],
                                                w["w_rT"][:, :], start=True, stop=True)
                    last.then_inc(r_in_psum, 1)
            pe.wait_ge(consts_set, 1)
            steps(pe, step, -1, NB)


def transformer_kernel(nc, a, out):
    E, HE = 8, 32
    ctx = ExitStack()
    with ctx:
        def sb(nm, shape, dt=F32):
            return ctx.enter_context(nc.sbuf_tensor(nm, shape, dt))

        x_sb = sb("x_sb", [P, NB * NT * D])
        loading = {nm: ctx.enter_context(nc.semaphore(f"{nm}_loaded")) for nm in ("x_first", "x_rest", "late")}
        w = {nm: sb(nm, shape) for nm, shape in (
            ("l0_bv", [P, P]), ("bd1", [P, NT, E * HE]), ("l0_bq_scaled", [P, 1]))}
        packed = {part: sb(f"w_{part}", list(a["w_" + part].shape)) for part in ("first", "late")}
        for part, tile in packed.items():
            at = 0
            for nm, shape in a["_" + part]:
                n = int(np.prod(shape[1:]))
                view = tile[:, at:at + n]
                if len(shape) == 3:
                    view = view.rearrange("p (a b) -> p a b", a=shape[1])
                if len(shape) == 4:
                    view = view.rearrange("p (a b c) -> p a b c", a=shape[1], b=shape[2])
                w[nm] = view
                at += n
        w["ident_bf"] = sb("ident_bf", [P, P], BF16)
        w["mask"] = sb("mask", [P, 4, P], BF16)
        w["moment_weights"] = sb("moment_weights", [P, 2, 2 * P + 1])
        w["neg_expert"] = sb("neg_expert", [P, 2, E])
        w["twice_bd2T"] = sb("twice_bd2T", [P, E])
        w["neg_bias_loss"] = sb("neg_bias_loss", [1, E])

        inner = ExitStack()
        with inner:
            bd2T_sq = inner.enter_context(nc.sbuf_tensor("bd2T_sq", [P, E], F32))
            w2b2 = inner.enter_context(nc.sbuf_tensor("w2b2", [P, 2, E], F32))
            w2b2_sum = inner.enter_context(nc.sbuf_tensor("w2b2_sum", [P, 2], F32))
            ps = [inner.enter_context(nc.psum_tensor(f"setup{i}", [P, 512], F32)) for i in range(4)]
            loaded, squared, products, tables = (inner.enter_context(nc.semaphore(nm)) for nm in
                                                 ("loaded", "squared", "products", "tables"))
            block = inner.enter_context(nc.Block())
            loads = [(packed["first"][:, :], a["w_first"])]
            for nm in ("l0_bv", "bd1"):
                row = a[nm + "_row"]
                n = row.shape[1]
                dst = w[nm]
                if nm == "bd1":
                    loads += [(dst[:, t, :], row.partition_broadcast(P)) for t in range(NT)]
                else:
                    loads.append((dst[:, :], row.partition_broadcast(P)))
            x_v = a["x"].rearrange("(n p) d -> p n d", p=P)
            x_t = x_sb[:, :].rearrange("p (n d) -> p n d", d=D)
            first = X_FIRST * NT

            @block.sync
            def _(sp):
                sp.dma_start(*loads[0]).then_inc(loaded, 16)
                sp.dma_start(x_t[:, 0:first, :], x_v[:, 0:first, :]).then_inc(loading["x_first"], 16)

            @block.scalar
            def _(act):
                for dst, src in loads[1:]:
                    act.dma_start(dst, src).then_inc(loaded, 16)
                act.dma_start(x_t[:, first:, :], x_v[:, first:, :]).then_inc(loading["x_rest"], 16)
                act.dma_start(packed["late"][:, :], a["w_late"]).then_inc(loading["late"], 16)

            @block.vector
            def _(dve):
                dve.wait_ge(loaded, 16 * len(loads))
                nc.vector.tensor_tensor(bd2T_sq[:, :], w["bd2T"][:, :], w["bd2T"][:, :], ALU.mult)\
                    .then_inc(squared, 1)
                nc.vector.tensor_copy(w["ident_bf"][:, :], w["ident"][:, :])
                for i in range(4):
                    nc.vector.tensor_copy(w["mask"][:, i, :], w["mask_f"][:, :])
                nc.vector.tensor_scalar(w["l0_bq_scaled"][:, :], w["l0_bq"][:, :], float(HD) ** -0.5, None, ALU.mult)
                nc.vector.tensor_scalar(w["neg_expert"][:, :, :], w["expert_of"][:, :, :], -1.0, None, ALU.mult)
                nc.vector.tensor_scalar(w["twice_bd2T"][:, :], w["bd2T"][:, :], 2.0, None, ALU.mult)
                dve.wait_ge(products, 1)
                nc.vector.tensor_scalar(w["neg_bias_loss"][:, :], ps[3][0:1, 0:E], -float(T), None, ALU.mult)
                for g in range(2):
                    gram, cross, ones = ((0, P, 2 * P), (P + 1, 0, P))[g]
                    mw = w["moment_weights"]
                    nc.vector.tensor_tensor(mw[:, g, gram:gram + P], ps[g][:, 0:P], w["block_mask"][:, :], ALU.mult)
                    nc.vector.tensor_scalar(mw[:, g, cross:cross + P], w["wd2"][:, g, :], -2.0, None, ALU.mult)
                    nc.vector.tensor_tensor(w2b2[:, g, :], ps[2][:, g * E:(g + 1) * E], w["expert_of"][:, g, :],
                                            ALU.mult).then_inc(tables, 1)
                    dve.wait_ge(tables, 2 * g + 1)
                    nc.vector.tensor_reduce(out=w2b2_sum[:, g:g + 1], in_=w2b2[:, g, :], axis=AX.X, op=ALU.add)\
                        .then_inc(tables, 1)
                    dve.wait_ge(tables, 2 * g + 2)
                    nc.vector.tensor_scalar(mw[:, g, ones:ones + 1], w2b2_sum[:, g:g + 1], 2.0, None, ALU.mult)

            @block.tensor
            def _(pe):
                pe.wait_ge(loaded, 16 * len(loads))
                for g in range(2):
                    w2T = w["wd2T"][:, g * P:(g + 1) * P]
                    nc.tensor.matmul(ps[g][:, 0:P], w2T, w2T, start=True, stop=True)
                    nc.tensor.matmul(ps[2][:, g * E:(g + 1) * E], w2T, w["bd2T"][:, :], start=True, stop=True)
                pe.wait_ge(squared, 1)
                nc.tensor.matmul(ps[3][0:1, 0:E], w["ones"][:, :], bd2T_sq[:, :], start=True, stop=True)\
                    .then_inc(products, 1)

        shared = {nm: w[nm] for nm in ("ident", "ident_bf", "mask", "den_pick", "neghalf", "ones", "rope")}
        w["b_base_dram"] = a["b_base"]
        attention(nc, "a0", x_sb, loading,
                  shared | {nm[3:]: w[nm] for nm in w if nm.startswith("l0_")}, causal=False)
        expert_ffn(nc, x_sb, w, a["wa_down"], a["ba_down"], a["wa_up"], a["ba_up"])
        attention(nc, "a1", x_sb, None, shared | {nm[3:]: w[nm] for nm in w if nm.startswith("l1_")}, causal=True)
        channel_mix(nc, x_sb, w, out)


def kernel(**inputs):
    import numpy as np
    import concourse.bacc as _bacc
    from concourse.bass_utils import run_bass_kernel_spmd as _run

    i = {k: np.asarray(v) for k, v in inputs.items()}
    E, HE = 8, 32
    dh = np.arange(P).reshape(H, HD).T.reshape(-1)
    rot = np.arange(P).reshape(H, 2, HD // 2)[:, ::-1].reshape(-1)

    def padded_out(wT, bias=None):
        z = np.zeros((2, 4, 2, 16, P), wT.dtype)
        z[:, :, :, 0:HD] = wT.reshape(2, 4, 2, HD, P)
        if bias is not None:
            z[0, 0, 0, HD] = bias
        return z.reshape(2, P, P).transpose(1, 0, 2)

    w_in, wa = i["L0_attn_w_in"], i["L1_attn_W_attn"]
    arr = {
        "l0_wq": w_in[0:P][dh].T, "l0_wk": w_in[P:2 * P][dh].T, "l0_wv": w_in[2 * P:].T,
        "l0_wo": padded_out(i["L0_attn_w_out"].T, i["L0_attn_b_out"]),
        "l0_bq": i["L0_attn_b_in"][0:P][dh][:, None], "l0_bk": i["L0_attn_b_in"][P:2 * P][dh][:, None],
        "l1_wq": wa[:, 0:P][:, dh], "l1_wqrot": wa[:, 0:P][:, rot][:, dh],
        "l1_wk": wa[:, P:2 * P][:, dh], "l1_wkrot": wa[:, P:2 * P][:, rot][:, dh],
        "l1_wv": wa[:, 2 * P:], "l1_wo": padded_out(i["L1_attn_W_proj"]),
        "w_base": i["L0_ffn_W_base"],
        "wd1": i["L0_ffn_Wd1"].transpose(1, 0, 2).reshape(D, E * HE),
        "wd2": i["L0_ffn_Wd2"].reshape(2, P, D).transpose(1, 0, 2),
        "wd2T": i["L0_ffn_Wd2"].reshape(E * HE, D).T, "bd2T": i["L0_ffn_bd2"].T,
        "w_rT": i["L1_ffn_W_r"].T, "w_kT": i["L1_ffn_W_k"].T, "w_vT": i["L1_ffn_W_v"].T,
        "mu_r": i["L1_ffn_mu_r"][:, None], "mu_k": i["L1_ffn_mu_k"][:, None],
    }
    inv = (1.0 / 10000.0 ** (np.arange(0, HD, 2, dtype=np.float32) / HD)).astype(np.float32)
    freqs = np.arange(T, dtype=np.float32)[:, None] * inv[None, :]
    emb = np.concatenate([freqs, freqs], axis=-1).T
    sign = np.where(np.arange(HD) < HD // 2, -1.0, 1.0)[:, None]
    table = np.stack([np.cos(emb), np.sin(emb) * sign], axis=1).astype(np.float32)
    scale = np.float32(HD ** -0.5)
    rope = np.stack([table * scale, table], axis=1)
    own = np.arange(P)
    row = np.arange(P)[:, None]
    consts = {
        "rope": np.repeat(rope, H, axis=0),
        "ident": np.eye(P), "mask_f": np.where(own[None, :] > own[:, None], -2.0 ** 126, 0.0),
        "den_pick": (row == 16 * np.arange(H // 2)[None, :] + HD) * 1.0,
        "neghalf": np.full((P, NT), -0.5), "ones": np.ones((P, 1)),
        "block_mask": (row // HE == own[None, :] // HE) * 1.0,
        "expert_of": np.stack([(g * 4 + row // HE == np.arange(E)[None, :]) * 1.0 for g in range(2)], axis=1),
    }
    arr |= {k: v.astype(np.float32) for k, v in consts.items()}
    early = ("ident", "mask_f", "den_pick", "neghalf", "ones", "wd2", "wd2T", "bd2T", "block_mask", "expert_of")
    parts = {"_first": [nm for nm in arr if nm.startswith("l0_") or nm in early]}
    parts["_late"] = [nm for nm in arr if nm not in parts["_first"]]
    shapes = {part: [(nm, arr[nm].shape) for nm in names] for part, names in parts.items()}
    arr = {"w" + part: np.concatenate([arr[nm].reshape(P, -1) for nm in names], axis=1)
           for part, names in parts.items()}
    arr |= {"x": i["L0_attn_x"].reshape(NB * T, D), "l0_bv_row": i["L0_attn_b_in"][None, 2 * P:],
            "bd1_row": i["L0_ffn_bd1"].reshape(1, E * HE), "b_base": i["L0_ffn_b_base"][None, :],
            "wa_down": i["L0_ffn_Wa_down"].reshape(E * D, 64), "ba_down": i["L0_ffn_ba_down"].reshape(E * 64, 1),
            "wa_up": i["L0_ffn_Wa_up"].reshape(E * 64, D), "ba_up": i["L0_ffn_ba_up"]}

    nc = _bacc.Bacc("TRN2", target_bir_lowering=False, num_devices=1)
    arrays, aps = {}, dict(shapes)
    for name, v in arr.items():
        v = np.ascontiguousarray(v)
        arrays[f"in_{name}_dram"] = v
        aps[name] = nc.dram_tensor(f"in_{name}_dram", v.shape, mybir.dt.from_np(v.dtype), kind="ExternalInput").ap()
    out = nc.dram_tensor("out_0_dram", (NB * T, D), F32, kind="ExternalOutput").ap()
    transformer_kernel(nc, aps, out)
    r = _run(nc, [arrays], core_ids=[0])
    return r.results[0]["out_0_dram"].reshape(NB, T, D)
```
